# Optimizing a Trainium2 kernel written in Bass

```python
import numpy as np
import jax
import jax.numpy as jnp

def _softmax(x, axis=-1):
    return jax.nn.softmax(x, axis=axis)

def _gelu(x):
    return jax.nn.gelu(x, approximate=True)

def _silu(x):
    return jax.nn.silu(x)

def _sigmoid(x):
    return jax.nn.sigmoid(x)

def _layernorm(x, axis=-1, eps=1e-05):
    m = jnp.mean(x, axis=axis, keepdims=True)
    v = jnp.var(x, axis=axis, keepdims=True)
    return (x - m) / jnp.sqrt(v + eps)

def _scatter_add(tgt, idx, src, axis=0):
    return tgt.at[idx].add(src)

def _segment_sum(src, seg, n):
    return jax.ops.segment_sum(src, seg, n)
kernel_name = 'mk_vit_tower_cls_d1_tok_img256_r4_6ada4c'

def setup_inputs(seed: int=0):
    np.random.seed(seed)
    _w = jnp.asarray

    def _rec_inputs():
        import jax
        import jax.numpy as jnp
        _rk = jax.random.key(seed)
        x = -0.000596345 + 1.00056 * jax.random.normal(jax.random.fold_in(_rk, 1), (128, 64, 64, 3), jnp.float32)
        cls_tok = 0.02 * jax.random.normal(jax.random.fold_in(_rk, 5), (1, 1, 64), jnp.float32)
        return (x, cls_tok)
    x, cls_tok = _rec_inputs()

    def _L0_tok_setup():
        import jax, jax.numpy as jnp
        import numpy as np
        from jax import lax
        NEG_SLOPE = 0.01

        def leaky(v):
            return jnp.where(v >= 0, v, NEG_SLOPE * v)
        key = jax.random.key(seed)
        ks = jax.random.split(key, 12)
        B, H, W = (16, 64, 64)
        width, mx, my, L, nl = (32, 16, 16, 3, 4)
        scale = 1.0 / (width * width)
        return {'x': jax.random.normal(ks[0], (B, H, W, 3), jnp.float32), 'input_grid': jax.random.uniform(ks[1], (H, W, 2), jnp.float32), 'P_w': jax.random.normal(ks[2], (5, width), jnp.float32) * 0.3, 'P_b': jax.random.normal(ks[3], (width,), jnp.float32) * 0.05, 'spec_wr': jax.random.uniform(ks[4], (nl, width, width, mx, my), jnp.float32) * scale, 'spec_wi': jax.random.uniform(ks[5], (nl, width, width, mx, my), jnp.float32) * scale, 'conv_w': jax.random.normal(ks[6], (nl, width, width, L, L), jnp.float32) * 0.05, 'conv_b': jax.random.normal(ks[7], (nl, width), jnp.float32) * 0.05, 'Q1_w': jax.random.normal(ks[8], (width, width), jnp.float32) * 0.15, 'Q1_b': jax.random.normal(ks[9], (width,), jnp.float32) * 0.05, 'Q2_w': jax.random.normal(ks[10], (width, 1), jnp.float32) * 0.15, 'Q2_b': jax.random.normal(ks[11], (1,), jnp.float32) * 0.05}
    _L0_tok_all = _L0_tok_setup()
    _L0_tok_in = {k: v for k, v in _L0_tok_all.items() if k in ('input_grid', 'P_w', 'P_b', 'spec_wr', 'spec_wi', 'conv_w', 'conv_b', 'Q1_w', 'Q1_b', 'Q2_w', 'Q2_b')}
    del _L0_tok_all

    def _L0_attn_setup():
        import jax, jax.numpy as jnp
        import numpy as np
        import math
        NUM_HEADS = 8
        HEAD_SIZE = 32

        def get_alibi_slopes(n_heads):

            def pow2_slopes(n):
                start = 2.0 ** (-2.0 ** (-(math.log2(n) - 3)))
                ratio = start
                return [start * ratio ** i for i in range(n)]
            if math.log2(n_heads).is_integer():
                return np.array(pow2_slopes(n_heads), dtype=np.float32)
            cp2 = 2 ** math.floor(math.log2(n_heads))
            extra = pow2_slopes(2 * cp2)[0::2][:n_heads - cp2]
            return np.array(pow2_slopes(cp2) + extra, dtype=np.float32)
        ALIBI_SLOPES = jnp.asarray(get_alibi_slopes(NUM_HEADS))
        key = jax.random.key(seed)
        ks = jax.random.split(key, 6)
        B, T, C = (32, 128, 64)
        s = 1.0 / math.sqrt(C)
        return {'x': jax.random.normal(ks[0], (B, T, C), dtype=jnp.float32), 'Wq': jax.random.normal(ks[1], (C, NUM_HEADS * HEAD_SIZE), dtype=jnp.float32) * s, 'Wk': jax.random.normal(ks[2], (C, NUM_HEADS * HEAD_SIZE), dtype=jnp.float32) * s, 'Wv': jax.random.normal(ks[3], (C, NUM_HEADS * HEAD_SIZE), dtype=jnp.float32) * s, 'Wo': jax.random.normal(ks[4], (NUM_HEADS * HEAD_SIZE, C), dtype=jnp.float32) * s, 'bo': jax.random.normal(ks[5], (C,), dtype=jnp.float32) * 0.01}
    _L0_attn_all = _L0_attn_setup()
    _L0_attn_in = {k: v for k, v in _L0_attn_all.items() if k in ('Wq', 'Wk', 'Wv', 'Wo', 'bo')}
    del _L0_attn_all

    def _L0_ffn_setup():
        import jax, jax.numpy as jnp
        import numpy as np
        DIM = 64
        HEADS = 8
        NUM_KEYS = 64
        NUM_KV = NUM_KEYS ** 2
        PK_TOPK = 16
        FINAL_TOPK = 16
        DIM_KEY = DIM // 2
        P = 2

        def _pk(x, Wq_pk, pk_keys):
            b, n, _ = x.shape
            q = (x @ Wq_pk).reshape(b, n, P, HEADS, DIM_KEY).transpose(2, 0, 1, 3, 4)
            sim = jnp.einsum('pbnhd,pkhd->pbnhk', q, pk_keys)
            scores, idx = jax.lax.top_k(sim, PK_TOPK)
            idx0 = idx[0]
            idx1 = idx[1] * NUM_KEYS
            index = (idx0[..., :, None] + idx1[..., None, :]).reshape(b, n, HEADS, PK_TOPK * PK_TOPK)
            score = (scores[0][..., :, None] + scores[1][..., None, :]).reshape(b, n, HEADS, PK_TOPK * PK_TOPK)
            final_scores, pk_idx = jax.lax.top_k(score, FINAL_TOPK)
            final_indices = jnp.take_along_axis(index, pk_idx, axis=-1)
            final_scores = jax.nn.softmax(final_scores, axis=-1)
            return (final_scores, final_indices)
        key = jax.random.key(seed)
        ks = jax.random.split(key, 7)
        b, n = (2, 256)
        std = 0.02
        x = jax.random.normal(ks[0], (b, n, DIM), dtype=jnp.float32)
        Wq_pk = jax.random.normal(ks[1], (DIM, P * HEADS * DIM_KEY), dtype=jnp.float32) * std
        pk_keys = jax.random.normal(ks[2], (P, NUM_KEYS, HEADS, DIM_KEY), dtype=jnp.float32) * std
        Wq = jax.random.normal(ks[3], (DIM, HEADS * DIM), dtype=jnp.float32) * std
        keys_table = jax.random.normal(ks[4], (NUM_KV * HEADS, DIM), dtype=jnp.float32) * std
        values_table = jax.random.normal(ks[5], (NUM_KV * HEADS, DIM), dtype=jnp.float32) * std
        Wo = jax.random.normal(ks[6], (DIM * HEADS, DIM), dtype=jnp.float32) * std
        return {'x': x, 'Wq_pk': Wq_pk, 'pk_keys': pk_keys, 'Wq': Wq, 'keys_table': keys_table, 'values_table': values_table, 'Wo': Wo}
    _L0_ffn_all = _L0_ffn_setup()
    _L0_ffn_in = {k: v for k, v in _L0_ffn_all.items() if k in ('Wq_pk', 'pk_keys', 'Wq', 'keys_table', 'values_table', 'Wo')}
    del _L0_ffn_all
    return {'x': x, 'cls_tok': cls_tok, 'L0_tok_input_grid': _L0_tok_in['input_grid'], 'L0_tok_P_w': _L0_tok_in['P_w'], 'L0_tok_P_b': _L0_tok_in['P_b'], 'L0_tok_spec_wr': _L0_tok_in['spec_wr'], 'L0_tok_spec_wi': _L0_tok_in['spec_wi'], 'L0_tok_conv_w': _L0_tok_in['conv_w'], 'L0_tok_conv_b': _L0_tok_in['conv_b'], 'L0_tok_Q1_w': _L0_tok_in['Q1_w'], 'L0_tok_Q1_b': _L0_tok_in['Q1_b'], 'L0_tok_Q2_w': _L0_tok_in['Q2_w'], 'L0_tok_Q2_b': _L0_tok_in['Q2_b'], 'L0_attn_Wq': _L0_attn_in['Wq'], 'L0_attn_Wk': _L0_attn_in['Wk'], 'L0_attn_Wv': _L0_attn_in['Wv'], 'L0_attn_Wo': _L0_attn_in['Wo'], 'L0_attn_bo': _L0_attn_in['bo'], 'L0_ffn_Wq_pk': _L0_ffn_in['Wq_pk'], 'L0_ffn_pk_keys': _L0_ffn_in['pk_keys'], 'L0_ffn_Wq': _L0_ffn_in['Wq'], 'L0_ffn_keys_table': _L0_ffn_in['keys_table'], 'L0_ffn_values_table': _L0_ffn_in['values_table'], 'L0_ffn_Wo': _L0_ffn_in['Wo']}

def reference(x, cls_tok, L0_tok_input_grid, L0_tok_P_w, L0_tok_P_b, L0_tok_spec_wr, L0_tok_spec_wi, L0_tok_conv_w, L0_tok_conv_b, L0_tok_Q1_w, L0_tok_Q1_b, L0_tok_Q2_w, L0_tok_Q2_b, L0_attn_Wq, L0_attn_Wk, L0_attn_Wv, L0_attn_Wo, L0_attn_bo, L0_ffn_Wq_pk, L0_ffn_pk_keys, L0_ffn_Wq, L0_ffn_keys_table, L0_ffn_values_table, L0_ffn_Wo):
    import jax
    import jax.numpy as jnp

    def _L0_tok_ref(x, input_grid, P_w, P_b, spec_wr, spec_wi, conv_w, conv_b, Q1_w, Q1_b, Q2_w, Q2_b):
        import jax, jax.numpy as jnp
        import numpy as np
        from jax import lax
        NEG_SLOPE = 0.01

        def leaky(v):
            return jnp.where(v >= 0, v, NEG_SLOPE * v)
        B, H, W, _ = x.shape
        nl, _, _, mx, my = spec_wr.shape
        grid = jnp.broadcast_to(input_grid[None], (B, H, W, input_grid.shape[-1]))
        h = jnp.concatenate([grid, x], axis=-1) @ P_w + P_b
        h = jnp.transpose(h, (0, 3, 1, 2))
        dn = ('NCHW', 'OIHW', 'NCHW')
        for i in range(nl):
            h_ft = jnp.fft.rfft2(h)
            w_c = spec_wr[i] + 1j * spec_wi[i]
            out_modes = jnp.einsum('bixy,ioxy->boxy', h_ft[:, :, :mx, :my], w_c)
            spec = jnp.fft.irfft2(out_modes, s=(H, W))
            conv = lax.conv_general_dilated(h, conv_w[i], (1, 1), 'SAME', dimension_numbers=dn)
            conv = conv + conv_b[i][None, :, None, None]
            h = leaky(spec + conv)
        h = jnp.transpose(h, (0, 2, 3, 1))
        h = leaky(h @ Q1_w + Q1_b)
        out = (h @ Q2_w + Q2_b)[..., 0]
        return out

    def _L0_attn_ref(x, Wq, Wk, Wv, Wo, bo):
        import jax, jax.numpy as jnp
        import numpy as np
        import math
        NUM_HEADS = 8
        HEAD_SIZE = 32

        def get_alibi_slopes(n_heads):

            def pow2_slopes(n):
                start = 2.0 ** (-2.0 ** (-(math.log2(n) - 3)))
                ratio = start
                return [start * ratio ** i for i in range(n)]
            if math.log2(n_heads).is_integer():
                return np.array(pow2_slopes(n_heads), dtype=np.float32)
            cp2 = 2 ** math.floor(math.log2(n_heads))
            extra = pow2_slopes(2 * cp2)[0::2][:n_heads - cp2]
            return np.array(pow2_slopes(cp2) + extra, dtype=np.float32)
        ALIBI_SLOPES = jnp.asarray(get_alibi_slopes(NUM_HEADS))
        B, T, C = x.shape
        H, D = (NUM_HEADS, HEAD_SIZE)
        q = (x @ Wq).reshape(B, T, H, D).transpose(0, 2, 1, 3)
        k = (x @ Wk).reshape(B, T, H, D).transpose(0, 2, 1, 3)
        v = (x @ Wv).reshape(B, T, H, D).transpose(0, 2, 1, 3)
        scale = 1.0 / math.sqrt(D)
        wei = jnp.einsum('bhtd,bhsd->bhts', q, k) * scale
        pos = jnp.arange(T)
        rel = (pos[None, :] - pos[:, None]).astype(jnp.float32)
        bias = ALIBI_SLOPES[:, None, None] * rel[None, :, :]
        wei = wei + bias[None]
        causal = pos[None, :] <= pos[:, None]
        wei = jnp.where(causal[None, None], wei, -jnp.inf)
        wei = jax.nn.softmax(wei, axis=-1)
        out = jnp.einsum('bhts,bhsd->bhtd', wei, v)
        out = out.transpose(0, 2, 1, 3).reshape(B, T, H * D)
        return out @ Wo + bo

    def _L0_ffn_ref(x, Wq_pk, pk_keys, Wq, keys_table, values_table, Wo):
        import jax, jax.numpy as jnp
        import numpy as np
        DIM = 64
        HEADS = 8
        NUM_KEYS = 64
        NUM_KV = NUM_KEYS ** 2
        PK_TOPK = 16
        FINAL_TOPK = 16
        DIM_KEY = DIM // 2
        P = 2

        def _pk(x, Wq_pk, pk_keys):
            b, n, _ = x.shape
            q = (x @ Wq_pk).reshape(b, n, P, HEADS, DIM_KEY).transpose(2, 0, 1, 3, 4)
            sim = jnp.einsum('pbnhd,pkhd->pbnhk', q, pk_keys)
            scores, idx = jax.lax.top_k(sim, PK_TOPK)
            idx0 = idx[0]
            idx1 = idx[1] * NUM_KEYS
            index = (idx0[..., :, None] + idx1[..., None, :]).reshape(b, n, HEADS, PK_TOPK * PK_TOPK)
            score = (scores[0][..., :, None] + scores[1][..., None, :]).reshape(b, n, HEADS, PK_TOPK * PK_TOPK)
            final_scores, pk_idx = jax.lax.top_k(score, FINAL_TOPK)
            final_indices = jnp.take_along_axis(index, pk_idx, axis=-1)
            final_scores = jax.nn.softmax(final_scores, axis=-1)
            return (final_scores, final_indices)
        b, n, d = x.shape
        q = (x @ Wq).reshape(b, n, HEADS, DIM) * DIM ** (-0.5)
        kv_scores, indices = _pk(x, Wq_pk, pk_keys)
        offsets = jnp.arange(HEADS, dtype=indices.dtype) * NUM_KV
        ind = indices + offsets[None, None, :, None]
        k = jnp.einsum('bnhk,bnhkd->bnhd', kv_scores, keys_table[ind])
        v = jnp.einsum('bnhk,bnhkd->bnhd', kv_scores, values_table[ind])
        sim = jnp.einsum('bihd,bjhd->bhij', q, k)
        neg = -jnp.finfo(sim.dtype).max
        causal = jnp.tril(jnp.ones((n, n), dtype=bool))
        sim = jnp.where(causal, sim, neg)
        attn = jax.nn.softmax(sim, axis=-1)
        out = jnp.einsum('bhij,bjhd->bhid', attn, v)
        out = out.transpose(0, 2, 1, 3).reshape(b, n, HEADS * DIM)
        return out @ Wo
    h = _L0_tok_ref(x, L0_tok_input_grid, L0_tok_P_w, L0_tok_P_b, L0_tok_spec_wr, L0_tok_spec_wi, L0_tok_conv_w, L0_tok_conv_b, L0_tok_Q1_w, L0_tok_Q1_b, L0_tok_Q2_w, L0_tok_Q2_b)
    h = jnp.concatenate([jnp.broadcast_to(cls_tok, (h.shape[0], 1, h.shape[2])), h], axis=1)
    h = h + _L0_attn_ref(_layernorm(h, axis=-1), L0_attn_Wq, L0_attn_Wk, L0_attn_Wv, L0_attn_Wo, L0_attn_bo)
    h = h + _L0_ffn_ref(_layernorm(h, axis=-1), L0_ffn_Wq_pk, L0_ffn_pk_keys, L0_ffn_Wq, L0_ffn_keys_table, L0_ffn_values_table, L0_ffn_Wo)
    return h

_drawn_inputs = setup_inputs


def setup_inputs(seed=0):
    import zlib

    import numpy as np

    out = dict(_drawn_inputs(seed))
    spreads = {}
    factors = {'L0_tok_spec_wr': 8.0,
     'L0_tok_spec_wi': 8.0,
     'L0_attn_bo': 4.445,
     'L0_ffn_Wq_pk': 8.0,
     'L0_ffn_pk_keys': 8.0,
     'L0_ffn_Wq': 64.0,
     'L0_ffn_keys_table': 64.0,
     'L0_ffn_values_table': 8.0,
     'L0_ffn_Wo': 8.0}
    for name, (base, spread) in spreads.items():
        noise = np.random.default_rng([zlib.crc32(name.encode()), seed]).standard_normal(out[name].shape)
        drawn = base * np.exp(spread * noise) if base else spread * noise
        out[name] = jnp.asarray(drawn.astype(out[name].dtype))
    for name, factor in factors.items():
        out[name] = (out[name] * factor).astype(out[name].dtype)
    return out
```

```python
from contextlib import ExitStack

import numpy as np

import concourse.bass as bass
from concourse import mybir

F32 = mybir.dt.float32
U32 = mybir.dt.uint32
ALU = mybir.AluOpType
ACT = mybir.ActivationFunctionType
AX = mybir.AxisListType

IMGS = 128
SIDE = 64
CH = 32
LAYERS = 4
MODES = 16
GROUP = 8
GROUPS = IMGS // GROUP
PAIRS = GROUP // 2
STAGES = LAYERS + 1
UNITS = STAGES * GROUP
BLK = SIDE // 2
PITCH = BLK + 1
HA_LEN = BLK * PITCH
OFF_LEN = PITCH * PITCH + 1
HM = 128
WCH = 16
NWCH = HM // WCH
WRING = 2
H = 8
D1 = 32
D2 = 64
KEYS = 64
TOP = 16
ROWS = H * KEYS * KEYS
SPAN = 10
HALF = TOP // 2
GRING = 3
EPS = 1e-5
SLOPE = 0.01
NEG = -1e30
LOW = -3e38
CAND = [(0, 1, 16), (1, 1, 8), (2, 1, 5), (3, 1, 4), (4, 1, 3), (5, 3, 2), (8, 8, 1)]
NCAND = sum(n * b for _, n, b in CAND)

R_LN1, R_XT1, R_QKV, R_SC1, R_PT1, R_PV1, R_AOT, R_WO1, R_XT2, R_QPK = range(10)
R_SIM, R_TOP0, R_TOP1, R_CAND, R_SOFT = range(10, 15)
R_DEC = {15: (0, 3), 16: (3, 6), 17: (6, 8)}
R_SUM = {18: (0, 2), 19: (2, 4), 20: (4, 6), 21: (6, 8), 22: (8, 9), 23: (9, 11), 24: (11, 13), 25: (13, 15), 26: (15, 16)}
R_KT, R_SC2, R_PT2, R_PV2, R_FOT, R_WO2, R_OUT = range(27, 34)


def tower_kernel(nc, x12, grid8, pw, pb, wl, cwt, cb, q1w, q1b, q2w, q2b, cls, wq, wk, wv, wo,
                 bo, wqpk, keyst, wq2, table, wo2, ft_c, i1_c, i2_c, ident_c, rel_c, relcls_c,
                 iota_c, head_c, out):
    ctx = ExitStack()
    with ctx:
        def sb(name, shape, dt=F32):
            return ctx.enter_context(nc.sbuf_tensor(name, shape, dt))

        def pb_(name):
            return ctx.enter_context(nc.psum_tensor(name, [128, 512], F32))

        def sem(name):
            return ctx.enter_context(nc.semaphore(name))

        wmix = nc.dram_tensor("wmix", (LAYERS, 128, HM * 2 * CH), F32, kind="Internal").ap()
        rows = nc.dram_tensor("rows", (IMGS * SIDE, SIDE), F32, kind="Internal").ap()

        off = sb("off", [128, GROUP, OFF_LEN])
        ha = sb("ha", [128, 2, HA_LEN])
        fold1 = sb("fold1", [128, 16, BLK])
        fold = sb("fold", [128, 2, 2, 16, 16])
        qh = fold[:, :, :, :, :].rearrange("c p q y x -> c (p q y x)")
        tt = sb("tt", [128, 8, 4, 4, CH])
        zz = sb("zz", [128, HM, GROUP])
        mx = sb("mx", [128, GROUP, HM])
        wr = sb("wr", [128, WRING, WCH * 2 * CH])
        mt = sb("mt", [128, 4, 2, CH])
        vt = sb("vt", [128, 4, 2, CH])
        vs = sb("vs", [128, 2, 2, 8, 2, CH])
        ft = sb("ft", [128, 4 * 8, 128])
        i1 = sb("i1", [128, 32, 128])
        i2 = sb("i2", [128, 2, 128])
        ident = sb("ident", [128, 128])
        cw = sb("cw", [128, LAYERS, 4, 128])
        lw = sb("lw", [128, 128])
        q1 = sb("q1", [128, 128])
        q2 = sb("q2", [128, 34])
        bias = sb("bias", [128, 8])
        xl = vs[:, :, :, :, :, :].rearrange("k s i a b c -> k s (i a b c)")
        rr = tt[0:2, :, :, :, :].rearrange("k a b i c -> k (a b i c)")[:, 0:2048]

        ht = sb("ht", [128, 4, SIDE])
        h1 = sb("h1", [128, 4, SIDE])
        lnst = sb("lnst", [128, 2, 6 + 4])
        xn = sb("xn", [128, SIDE])
        xnt = sb("xnt", [128, 128])
        qt = sb("qt", [128, 2, 128])
        kb = sb("kb", [128, 2, 4, 128])
        vv = sb("vv", [128, H, D1])
        ee = sb("ee", [128, H, 129])
        pt = sb("pt", [128, H, 128])
        fo = sb("fo", [128, H, D2])
        ao = fo[:, :, :].rearrange("t h d -> t (h d)")[:, 0:H * D1].rearrange("t (h d) -> t h d", h=H)
        rest = sb("rest", [128, H, KEYS])
        ftmp = rest
        atmp = ftmp[:, :, :].rearrange("t h d -> t (h d)")[:, 0:H * D1].rearrange("t (h d) -> t h d", h=H)
        aot = sb("aot", [128, 4, 128])
        smx = sb("smx", [128, 2, 4, H])
        qk = sb("qk", [128, 4, 128])
        fq = sb("fq", [128, 2, 4, 128])
        sim = ee[:, :, :].rearrange("t h s -> t (h s)")[:, 0:1024].rearrange("t (g k) -> t g k", k=KEYS)
        hot = ee[:, :, :].rearrange("t h s -> t (h s)")[:, 0:TOP * NCAND].rearrange("t (k c) -> t k c", k=TOP)
        tv = sb("tv", [128, 2, H, TOP])
        ti = sb("ti", [128, 2, H, TOP], U32)
        tf = sb("tf", [128, 2, H, TOP])
        cs = fo[:, :, 0:NCAND]
        ci_ = sb("ci", [128, H, NCAND])
        fv = sb("fv", [128, H, TOP])
        fp = sb("fp", [128, H, TOP], U32)
        crest = rest[:, :, 0:NCAND]
        pwt = sb("pwt", [128, 2, H, TOP])
        psm = sb("psm", [128, 2, H])
        fx = tf[:, 0, :, :]
        ix = sb("ix", [128, 2, H, TOP], U32)
        gg = sb("gg", [128, GRING, HALF, 128])
        kv = sb("kv", [128, 2, H, D2])
        kvh = sb("kvh", [128, 2, D2])
        vf = sb("vf", [128, H, D2])
        ob = sb("ob", [128, 2, SIDE])
        wqs = sb("wqs", [128, 3, H * D1])
        wos = sb("wos", [128, 2, SIDE])
        bob = sb("bob", [128, SIDE])
        wpks = sb("wpks", [128, 512])
        keyb = sb("keyb", [128, 4, 256])
        wq2s = sb("wq2s", [128, 512])
        wo2s = sb("wo2s", [128, 4, SIDE])
        rel = sb("rel", [128, 128])
        relcls = sb("relcls", [128, H])
        mask = sb("mask", [128, 128])
        iota = sb("iota", [128, NCAND])
        headoff = sb("headoff", [128, H])
        k0b = sb("k0b", [128, 2, 4])
        v0 = sb("v0", [128, H, D1])
        kcb = sb("kcb", [128, 4, 2])
        vc = sb("vc", [128, H, D2])

        cvb = [pb_("cv0"), pb_("cv1")]
        tpb = pb_("tp")
        b3 = pb_("b3")
        b4 = pb_("b4")
        b5 = pb_("b5")
        wide = ctx.enter_context(nc.psum_tensor("wide", [128, 1024], F32))


        s_zero, s_const = sem("zeroed"), sem("constants_in")
        s_wi, s_neg, s_ws = sem("wi_in"), sem("wi_negated"), sem("wmix_out")
        s_grid = sem("grid_in")
        s_xl = [sem("pixels_in0"), sem("pixels_in1")]
        s_conv, s_lin, s_act = sem("conv_done"), sem("biased"), sem("rectified")
        s_fst, s_fold = sem("fold_y_done"), sem("fold_ready")
        s_off = [sem(f"offset_ready{i}") for i in range(GROUP)]
        s_tr, s_tt = sem("transposed"), sem("transposed_ready")
        s_fft, s_za, s_zd = sem("modes_done"), sem("modes_ready_even"), sem("modes_ready_odd")
        s_w = [sem(f"weights_in{i}") for i in range(WRING)]
        s_wchunk, s_mx = sem("weights_used"), sem("mixed_ready")
        s_it, s_mt, s_v, s_vt, s_vs = (sem("mode_rows_done"), sem("mode_rows_ready"), sem("inv_y_done"),
                                       sem("inv_y_odd_ready"), sem("inv_y_ready"))
        s_q1, s_ql, s_qh, s_q2, s_rr, s_rows = (sem("hidden_done"), sem("hidden_biased"), sem("hidden_ready"), sem("head_done"),
                                          sem("rows_ready"), sem("rows_out"))
        s_ht = [sem(f"tokens_in{i}") for i in range(PAIRS)]
        s_ln, s_sd, s_xn, s_xtp, s_xt = (sem("ln_steps"), sem("std_ready"), sem("normed"), sem("normed_t_done"),
                                         sem("normed_t_ready"))
        s_qkp, s_qka, s_qkd = sem("qkv_done"), sem("qk_ready"), sem("v_ready")
        s_scp, s_sm1, s_ex1, s_ptp, s_pt = (sem("scores1_done"), sem("softmax1_steps"), sem("exp1_ready"),
                                            sem("probs1_t_done"), sem("probs1_t_ready"))
        s_pvp, s_ao, s_aop, s_aot, s_wop, s_h1 = (sem("pv1_done"), sem("attn1_steps"), sem("attn1_t_done"),
                                                  sem("attn1_t_ready"), sem("wo1_done"), sem("h1_steps"))
        s_qpp, s_qp, s_fq, s_smp, s_sim = (sem("qpk_done"), sem("qpk_ready"), sem("fq_ready"), sem("sim_done"),
                                           sem("sim_ready"))
        s_top, s_cst, s_pws, s_pwe, s_dst = (sem("top_steps"), sem("cand_steps"), sem("weight_steps"),
                                             sem("weight_exp"), sem("decode_steps"))
        s_g = [sem(f"gathered{i}") for i in range(2 * H)]
        s_mul, s_red, s_kv = sem("rows_weighted"), sem("rows_summed"), sem("kv_ready")
        s_vf, s_ktp, s_kt = sem("values_ready"), sem("keys_t_done"), sem("keys_t_ready")
        s_sc2, s_sm2, s_ex2, s_pt2p, s_pt2 = (sem("scores2_done"), sem("softmax2_steps"), sem("exp2_ready"),
                                              sem("probs2_t_done"), sem("probs2_t_ready"))
        s_pv2, s_fo, s_fop, s_fot, s_wo2, s_ob = (sem("pv2_done"), sem("attn2_steps"), sem("attn2_t_done"),
                                                  sem("attn2_t_ready"), sem("wo2_done"), sem("rows_final"))
        s_out = [sem("out_even"), sem("out_odd")]
        n_const = [0]

        s_met = {k: sem(f"wait_met_{k}") for k in ("pe", "dve", "pool")}

        def held(engine, name):
            engine.sem_inc(s_met[name], 1)

        U2 = 2 * UNITS
        A2 = 2 * LAYERS * GROUP
        FOLDS = LAYERS * GROUP
        QUADS = LAYERS * 2
        CHUNKS = LAYERS * NWCH
        PI = LAYERS * PAIRS
        LN, SM, TOPS, CS, PW, DEC = 6, 6, 8, 8, 4, 27

        def static(it):
            return isinstance(it, int)

        def tile_no(it, j):
            return 0 if static(it) and it == 0 else PAIRS * it + (j - PAIRS + 1)

        def tiles(it, u, tail):
            for j in range(-3, PAIRS):
                r = u - SPAN * j
                if not 0 <= r <= R_OUT:
                    continue
                if static(it) and (it == 0 and j != 0 or it == 1 and j < 0) or tail and j >= 0:
                    continue
                yield j, r, static(it) and it == 0

        def older(it, j, k):
            return tile_no(it, j) - k >= 1 if static(it) else True

        def younger(it, j, k):
            return it > 0 and tile_no(it, j) + k <= IMGS // 2 if static(it) else True

        def iterations(engine, body):
            body(0, UNITS, True, False)
            body(1, UNITS, True, False)
            with engine.Fori(2, GROUPS) as it:
                body(it, UNITS, True, False)
            body(GROUPS, UNITS, False, False)
            body(GROUPS + 1, R_OUT - SPAN + 1, False, True)

        def image_ready(engine, it, u):
            if u < GROUP:
                engine.wait_ge(s_lin, U2 * it + 2 * u + 2)
            else:
                engine.wait_ge(s_act, A2 * it + 2 * (u - GROUP) + 2)

        def first(it):
            return static(it) and it == 0

        block = ctx.enter_context(nc.Block())

        @block.sync
        def _(sp):
            def const(dst, src):
                n_const[0] += 1
                sp.dma_start(dst, src).then_inc(s_const, 16)

            def col(v):
                return v.rearrange("(a b) -> a b", b=1)

            def row(v, n):
                return v.rearrange("(a b) -> a b", a=1).to_broadcast([128, n])

            sp.wait_ge(s_zero, 1)
            stage = tt[:, :, :, :, :].rearrange("k a b i c -> k (a b i c)")
            quarter = [(l, p, 64 * (l % 2) + 32 * p) for l in range(2) for p in range(2)]
            for c in range(4):
                if c:
                    sp.wait_ge(s_ws, 16 * 4 * c)
                cols = slice(HM * CH * (c % 2), HM * CH * (c % 2 + 1))
                for l, p, k in quarter:
                    sp.dma_start(stage[k:k + 32, :], wl[2 * (c // 2) + l, 64 * p + 32:64 * p + 64, cols]).then_inc(s_wi, 16)
                if c == 0:
                    const(ft[:, :, :], ft_c)
                    const(ident[:, :], ident_c)
                    for n, src in enumerate([pb] + [cb[l] for l in range(LAYERS)] + [q1b]):
                        for k in range(4):
                            const(bias[CH * k:CH * k + CH, n:n + 1], col(src))
                    for k in range(2):
                        const(bias[k:k + 1, 6:7], col(q2b))
                        const(bias[32 + k:33 + k, 6:7], col(q2b))
                    for k in range(4):
                        px, py = divmod(k, 2)
                        const(lw[3 * k:3 * k + 3, CH * k:CH * k + CH], pw[2:5, :])
                        const(lw[12 + 2 * k:14 + 2 * k, CH * k:CH * k + CH], pw[0:2, :])
                        const(q1[CH * k:CH * k + CH, CH * k:CH * k + CH], q1w)
                        const(q2[CH * k:CH * k + CH, 32 * px + py:32 * px + py + 1], q2w)
                    axis = [(u, o, a, 2 * u + o - a) for u in range(2) for o in range(2) for a in range(2)
                            if 0 <= 2 * u + o - a <= 2]
                    for u, qy, py, ty in axis:
                        for v, qx, px, tx in axis:
                            r0, c0 = 64 * qx + 32 * qy, 64 * px + 32 * py
                            const(cw[r0:r0 + 32, :, 2 * u + v, c0:c0 + 32], cwt[ty, tx])
                sp.wait_ge(s_neg, c + 1)
                for l, p, k in quarter:
                    sp.dma_start(wmix[2 * (c // 2) + l, 64 * p + 32:64 * p + 64, cols], stage[k:k + 32, :]).then_inc(s_ws, 16)
            for l in range(LAYERS):
                for p in range(2):
                    sp.dma_start(wmix[l, 64 * p:64 * p + 32, :], wl[l, 64 * p:64 * p + 32, :]).then_inc(s_ws, 16)
            const(i1[:, :, :], i1_c)
            const(i2[:, :, :], i2_c)
            for n, w in enumerate((wq, wk, wv)):
                const(wqs[0:SIDE, n, :], w)
            const(wos[:, :, :], wo.rearrange("(c k) n -> k c n", k=128))
            const(bob[:, :], row(bo, SIDE))
            const(wpks[0:SIDE, :], wqpk)
            const(wq2s[0:SIDE, :], wq2)
            const(wo2s[:, :, :], wo2.rearrange("(c k) n -> k c n", k=128))
            for p in range(2):
                for h in range(H):
                    k = h % 4
                    const(keyb[32 * k:32 * k + 32, 2 * p + h // 4, KEYS * k:KEYS * k + KEYS], keyst[p, h])
            const(rel[:, :], rel_c[0])
            const(mask[:, :], rel_c[1])
            const(relcls[:, :], relcls_c)
            const(iota[:, :], iota_c)
            const(headoff[:, :], head_c)
            const(ht[:, 0, :], cls.rearrange("a b c -> (a b) c").to_broadcast([128, SIDE]))
            sp.wait_ge(s_ws, 16 * (16 + 2 * LAYERS))

            def chunk(it, k):
                s, c = divmod(k, NWCH)
                if not (first(it) and k < WRING):
                    sp.wait_ge(s_wchunk, CHUNKS * it + (k - WRING + 1))
                sp.dma_start(wr[:, k % WRING, :], wmix[s, :, c * WCH * 2 * CH:(c + 1) * WCH * 2 * CH]).then_inc(s_w[k % WRING], 16)

            def pixels(it, i):
                if i >= 2:
                    sp.wait_ge(s_conv, U2 * it + 2 * (i - 1))
                sp.dma_start(xl[0:12, i % 2, :], x12[GROUP * it + i]).then_inc(s_xl[i % 2], 16)

            def out_rows(it, i):
                sp.wait_ge(s_rr, 2 * GROUP * it + 2 * i + 2)
                r0 = (GROUP * it + i) * SIDE
                sp.dma_start(rows[bass.ds(r0, SIDE), :].rearrange("(y p) x -> p y x", p=2),
                             rr.rearrange("p (y x) -> p y x", x=SIDE)).then_inc(s_rows, 16)
                if i % 2:
                    j = i // 2
                    sp.wait_ge(s_rows, 16 * GROUP * it + 16 * (i + 1))
                    if not (first(it) and j > 0):
                        sp.wait_ge(s_h1, 2 * tile_no(it, j) + 2)
                    sp.dma_start(ht[:, j, :], rows[bass.ds((GROUP * it + i - 1) * SIDE, 2 * SIDE), :]).then_inc(s_ht[j], 16)

            def body(it, units, fno, tail):
                if fno:
                    if not first(it):
                        sp.wait_ge(s_conv, U2 * it)
                    for k in range(2):
                        sp.dma_start(xl[12:20, k, :], grid8).then_inc(s_grid, 16)
                    pixels(it, 0)
                    pixels(it, 1)
                for u in range(units):
                    s, i = divmod(u, GROUP)
                    if fno:
                        if i == 0 and s >= 1:
                            for c in range(WRING, NWCH):
                                chunk(it, NWCH * (s - 1) + c)
                        if i == 1 and s < LAYERS:
                            for c in range(WRING):
                                chunk(it, NWCH * s + c)
                        if s < LAYERS:
                            image_ready(sp, it, u)
                            for px in range(2):
                                for py in range(2):
                                    src = 64 * px + 32 * py
                                    dst = 64 * (1 - px) + 32 * (1 - py)
                                    at = py * PITCH + px
                                    sp.dma_start(off[dst:dst + 32, i, at:at + HA_LEN],
                                                 ha[src:src + 32, u % 2, :]).then_inc(s_off[i], 16)
                        if s == 0 and i + 2 < GROUP:
                            pixels(it, i + 2)
                        if s == LAYERS and i >= 1:
                            out_rows(it, i - 1)
                    for j, r, is_cls in tiles(it, u, tail):
                        if r == R_OUT:
                            m = tile_no(it, j)
                            sp.wait_ge(s_ob, m + 1)
                            if is_cls:
                                sp.dma_start(out[:, 0, :], ob[:, 0, :]).then_inc(s_out[0], 16)
                            else:
                                for e in range(2):
                                    sp.dma_start(out[2 * (m - 1) + e, 1:SIDE + 1, :],
                                                 ob[64 * e:64 * e + 64, j % 2, :]).then_inc(s_out[j % 2], 16)
                if fno:
                    out_rows(it, GROUP - 1)

            iterations(sp, body)
            sp.wait_ge(s_out[0], 16 + 32 * (IMGS // 4))
            sp.wait_ge(s_out[1], 32 * (IMGS // 4))
            sp.wait_ge(s_rows, 16 * IMGS)

        @block.gpsimd
        def _(pool):
            for t in (off[:, :, :], ha[:, :, :], cw[:, :, :, :], lw[:, :], q1[:, :], q2[:, :], kb[:, :, :, :], keyb[:, :, :],
                      k0b[:, :, :], kcb[:, :, :], xnt[:, :], wqs[:, :, :], wpks[:, :], wq2s[:, :], bias[:, 0:7]):
                last = pool.memset(t, 0.0)
            pool.memset(bias[:, 7:8], EPS).then_inc(s_zero, 1)

            def gathers(it, j):
                m = tile_no(it, j)
                for q in range(2 * H):
                    h, half = divmod(q, 2)
                    if half == 0:
                        group = next(g for g in R_DEC.values() if g[0] <= h < g[1])
                        if h == group[0]:
                            pool.wait_ge(s_dst, DEC * m + 3 * group[1] + list(R_DEC.values()).index(group) + 1)
                    if not (first(it) and q < GRING):
                        pool.wait_ge(s_red, 2 * H * m + (q - GRING + 1 if q >= GRING else -((2 * H - 1 - q) % GRING)))
                    held(pool, "pool")
                    for k in range(HALF):
                        at = HALF * half + k
                        pool.indirect_dma_start(
                            out=gg[:, q % GRING, k, :], out_offset=None, in_=table,
                            in_offset=bass.IndirectOffsetOnAxis(ap=ix[:, j % 2, h, at:at + 1], axis=0),
                        ).then_inc(s_g[q], 16)

            gathers(0, 0)
            with pool.Fori(1, GROUPS + 1) as it:
                for j in range(PAIRS):
                    gathers(it, j)

        @block.tensor
        def _(pe):
            pe.wait_ge(s_const, 16 * n_const[0])
            mm = nc.tensor.matmul

            def transpose(dst, src):
                return mm(dst, src, ident[:, :], start=True, stop=True, is_transpose=True)

            def conv(it, u, hb, between):
                s, i = divmod(u, GROUP)
                if not (first(it) and u == 0):
                    pe.wait_ge(s_lin, U2 * it + 2 * (u - 1) + hb + 1)
                if s == 0:
                    if hb == 0:
                        pe.wait_ge(s_grid, 32 * it + 32)
                        pe.wait_ge(s_xl[i % 2], 16 * 4 * it + 16 * (i // 2 + 1))
                    mm(cvb[hb][:, :], lw[0:20, :], xl[0:20, i % 2, 512 * hb:512 * hb + 512], start=True,
                       stop=True).then_inc(s_conv, 1)
                    between()
                    return
                if hb == 0:
                    pe.wait_ge(s_off[i], 64 * LAYERS * it + 64 * s)

                def tap(t):
                    a, b = divmod(t, 2)
                    at = (16 * hb + a) * PITCH + b
                    rhs = off[:, i, at:at + 16 * PITCH].rearrange("k (y x) -> k y x", x=PITCH)[:, :, 0:BLK]
                    return mm(cvb[hb][:, :].rearrange("k (y x) -> k y x", x=BLK), cw[:, s - 1, t, :], rhs,
                              start=(t == 0), stop=(t == 3))

                for t in range(3):
                    tap(t)
                between()
                if hb == 0:
                    pe.wait_ge(s_vs, 2 * PI * it + 8 * (s - 1) + 2 * (i // 2) + 2)
                for c in range(4):
                    for px in range(2):
                        mm(cvb[hb][64 * px:64 * px + 64, 128 * c:128 * c + 128],
                           vs[:, (i // 2) % 2, i % 2, 4 * hb + c, :, :].rearrange("k a c -> k (a c)"),
                           i2[:, px, :], start=False, stop=False, skip_group_check=True)
                last = tap(3)
                last.then_inc(s_conv, 1)

            def turn(it, u, hb):
                if hb == 0:
                    pe.wait_ge(s_fold, FOLDS * it + u + 1)
                if u == 0 and hb == 0:
                    if not first(it):
                        pe.wait_ge(s_rr, 2 * GROUP * it)
                else:
                    pe.wait_ge(s_tt, 2 * FOLDS * it + 2 * u + hb)
                for c in range(4):
                    cc = 4 * hb + c
                    src = fold[:, cc // 4, (cc // 2) % 2, 8 * (cc % 2):8 * (cc % 2) + 8, :].rearrange("k y x -> k (y x)")
                    last = transpose(tpb[:, 128 * c:128 * c + 128], src)
                last.then_inc(s_tr, 1)

            def fft(it, s, q):
                pe.wait_ge(s_tt, 2 * FOLDS * it + 2 * (GROUP * s + 4 * q + 3) + 2)
                if q == 1:
                    pe.wait_ge(s_za, QUADS * it + 2 * s + 1)
                    pe.wait_ge(s_zd, QUADS * it + 2 * s + 1)
                    if s >= 1:
                        pe.wait_ge(s_vs, 2 * PI * it + 8 * s)
                elif s >= 1:
                    pe.wait_ge(s_mt, PI * it + 4 * s)
                    pe.wait_ge(s_vs, 2 * PI * it + 8 * s - 1)
                for cl in range(4):
                    for a in range(2):
                        for b in range(4):
                            last = mm((b3, b4)[cl // 2][:, 128 * (cl % 2):128 * (cl % 2) + 128],
                                      tt[:, 2 * cl + a, b, :, :].rearrange("k i c -> k (i c)"),
                                      ft[:, 8 * cl + 4 * a + b, :], start=(a == 0 and b == 0), stop=(a == 1 and b == 3))
                last.then_inc(s_fft, 1)

            def mix(it, s):
                pe.wait_ge(s_za, QUADS * it + 2 * s)
                pe.wait_ge(s_zd, QUADS * it + 2 * s)
                if s >= 2:
                    pe.wait_ge(s_vs, 2 * PI * it + 8 * (s - 1))
                for c in range(NWCH):
                    k = NWCH * (s - 1) + c
                    if c == NWCH // 2:
                        pe.wait_ge(s_mx, QUADS * it + 2 * (s - 1) + 1)
                    pe.wait_ge(s_w[k % WRING], 16 * (CHUNKS // WRING) * it + 16 * (k // WRING + 1))
                    held(pe, "pe")
                    for w in range(WCH):
                        for p, bank in ((0, b3), (1, b4)):
                            at = GROUP * (WCH * (c % (NWCH // 2)) + w)
                            last = mm(bank[64 * p:64 * p + 64, at:at + GROUP],
                                      wr[64 * p:64 * p + 64, k % WRING, 2 * CH * w:2 * CH * (w + 1)],
                                      zz[64 * p:64 * p + 64, WCH * c + w, :], start=True, stop=True)
                    last.then_inc(s_wchunk, 1)

            def mode_rows(it, s, k):
                pe.wait_ge(s_mx, QUADS * it + 2 * s)
                if k:
                    pe.wait_ge(s_vs, 2 * PI * it + 8 * (s - 1) + 2 * k)
                for e in range(2):
                    last = transpose(b3[:, 128 * e:128 * e + 128], mx[:, 2 * k + e, :])
                last.then_inc(s_it, 1)

            def inv_y(it, s, k, half):
                bank = b3 if half else b4
                pe.wait_ge(s_mt, PI * it + 4 * (s - 1) + k + 1)
                if half == 0 and k:
                    pe.wait_ge(s_vs, 2 * PI * it + 8 * (s - 1) + 2 * k - 1)
                if half and k == 3 and s < LAYERS:
                    pe.wait_ge(s_za, QUADS * it + 2 * s + 1)
                for p in range(2):
                    for c in range(2):
                        for py in range(2):
                            at = 64 * (4 * p + 2 * c + py)
                            for ri in range(2):
                                last = mm(bank[:, at:at + 64], i1[:, 8 * (2 * p + ri) + 2 * (2 * half + c) + py, :],
                                          mt[:, 2 * p + ri, :, :].rearrange("k i c -> k (i c)"), start=(ri == 0), stop=(ri == 1))
                last.then_inc(s_v, 1)

            def hidden(it, i, hb):
                g = 2 * GROUP * it + 2 * i + hb
                image_ready(pe, it, LAYERS * GROUP + i)
                if i == 0 and hb == 0:
                    pe.wait_ge(s_tt, 2 * FOLDS * it + 2 * FOLDS)
                else:
                    pe.wait_ge(s_rr, g)
                rhs = ha[:, i % 2, 16 * hb * PITCH:16 * (hb + 1) * PITCH].rearrange("k (y x) -> k y x", x=PITCH)[:, :, 0:BLK]
                mm(tpb[:, :].rearrange("k (y x) -> k y x", x=BLK), q1[:, :], rhs, start=True, stop=True).then_inc(s_q1, 1)

            def scalars(it, i, hb):
                pe.wait_ge(s_qh, 2 * GROUP * it + 2 * i + hb + 1)
                mm(tpb[0:34, :], q2[:, :], qh[:, 512 * hb:512 * hb + 512], start=True, stop=True).then_inc(s_q2, 1)

            def nothing():
                pass

            def unit(it, u):
                s, i = divmod(u, GROUP)
                if s >= 1 and i == 0:
                    mix(it, s)
                    mode_rows(it, s, 0)
                    inv_y(it, s, 0, 0)
                    inv_y(it, s, 0, 1)
                head = s == LAYERS and i >= 1
                conv(it, u, 0, (lambda: hidden(it, i - 1, 0)) if head else nothing)
                if s < LAYERS and i == 5:
                    fft(it, s, 0)
                if s >= 1 and i < 6:
                    if i % 2 == 0:
                        mode_rows(it, s, i // 2 + 1)
                    elif i < 5:
                        inv_y(it, s, i // 2 + 1, 1)
                if head:
                    scalars(it, i - 1, 0)
                if s < LAYERS and i >= 1:
                    turn(it, u - 1, 0)
                conv(it, u, 1, (lambda: hidden(it, i - 1, 1)) if head else nothing)
                if s >= 1 and i < 6:
                    if i % 2 == 0:
                        inv_y(it, s, i // 2 + 1, 0)
                    elif i == 5:
                        inv_y(it, s, 3, 1)
                if head:
                    scalars(it, i - 1, 1)
                if s < LAYERS and i >= 1:
                    turn(it, u - 1, 1)

            def unit_end(it, u):
                s, i = divmod(u, GROUP)
                if i == GROUP - 1 and s < LAYERS:
                    turn(it, u, 0)
                    turn(it, u, 1)
                    fft(it, s, 1)
                if i == GROUP - 1 and s == LAYERS:
                    for hb in range(2):
                        hidden(it, i, hb)
                        scalars(it, i, hb)

            def tile(it, j, r, is_cls):
                m = tile_no(it, j)
                n = m - 1
                old = lambda k: older(it, j, k)
                young = lambda k: younger(it, j, k)
                if r in (R_XT1, R_XT2):
                    k = int(r == R_XT2)
                    pe.wait_ge(s_xn, 2 * m + k + 1)
                    if k == 0 and old(3):
                        pe.wait_ge(s_fot, m - 2)
                    if static(it) and m == 1:
                        pe.wait_ge(s_ob, 1)
                    if k == 1:
                        pe.wait_ge(s_h1, 2 * m + 2)
                        if old(2):
                            pe.wait_ge(s_sm2, SM * (n - 2) + 1)
                    held(pe, "pe")
                    transpose(b5[0:SIDE, 0:128], xn[:, :]).then_inc(s_xtp, 1)
                elif r == R_QKV:
                    pe.wait_ge(s_xt, 2 * m + 1)
                    if not is_cls:
                        pe.wait_ge(s_sim, m)
                    for c in range(2):
                        for w in range(2):
                            mm(wide[:, 256 * w + 128 * c:256 * w + 128 * c + 128], wqs[:, w, 128 * c:128 * c + 128],
                               xnt[:, :], start=True, stop=True)
                    mm(wide[:, 512:768], xnt[:, :], wqs[:, 2, :], start=True, stop=True).then_inc(s_qkp, 1)
                elif r == R_SC1 and not is_cls:
                    pe.wait_ge(s_qka, m + 1)
                    pe.wait_ge(s_qkd, m + 1)
                    if old(3):
                        pe.wait_ge(s_ob, m - 2)
                    for c in range(2):
                        mm(wide[:, 512 * c:512 * c + 512], qt[:, c, :], kb[:, c, :, :].rearrange("k h s -> k (h s)"),
                           start=True, stop=True)
                    for c in range(2):
                        last = mm(b5[:, 4 * c:4 * c + 4], qt[:, c, :], k0b[:, c, :], start=True, stop=True)
                    last.then_inc(s_scp, 1)
                elif r in (R_PT1, R_PT2) and not is_cls:
                    pe.wait_ge(s_ex1 if r == R_PT1 else s_ex2, n + 1)
                    for h in range(H):
                        last = transpose(wide[:, 128 * h:128 * h + 128], ee[:, h, 0:128])
                    last.then_inc(s_ptp if r == R_PT1 else s_pt2p, 1)
                elif r == R_PV1 and not is_cls:
                    pe.wait_ge(s_pt, n + 1)
                    for h in range(H):
                        last = mm(b5[:, D1 * h:D1 * h + D1], pt[:, h, :], vv[:, h, :], start=True, stop=True)
                    last.then_inc(s_pvp, 1)
                elif r == R_AOT:
                    if is_cls:
                        pe.wait_ge(s_qkd, 1)
                    else:
                        pe.wait_ge(s_ao, 3 * n + 3)
                    src = v0 if is_cls else ao
                    for c in range(2):
                        last = transpose(b5[:, 128 * c:128 * c + 128], src[:, 4 * c:4 * c + 4, :].rearrange("t h d -> t (h d)"))
                    last.then_inc(s_aop, 1)
                elif r == R_WO1:
                    pe.wait_ge(s_aot, m + 1)
                    if old(2):
                        pe.wait_ge(s_kt, m - 1)
                    for c in range(2):
                        last = mm(b5[:, 0:SIDE], aot[:, c, :], wos[:, c, :], start=(c == 0), stop=(c == 1))
                    last.then_inc(s_wop, 1)
                elif r == R_QPK:
                    pe.wait_ge(s_xt, 2 * m + 2)
                    if old(2):
                        pe.wait_ge(s_pt2, n - 1)
                    for c in range(4):
                        mm(wide[:, 128 * c:128 * c + 128], wpks[:, 128 * c:128 * c + 128], xnt[:, :], start=True, stop=True)
                    for c in range(4):
                        last = mm(wide[:, 512 + 128 * c:640 + 128 * c], wq2s[:, 128 * c:128 * c + 128], xnt[:, :],
                                  start=True, stop=True)
                    last.then_inc(s_qpp, 1)
                elif r == R_SIM:
                    pe.wait_ge(s_qp, m + 1)
                    pe.wait_ge(s_fq, m + 1)
                    for c in range(4):
                        last = mm(wide[:, 256 * c:256 * c + 256], qk[:, c, :], keyb[:, c, :], start=True, stop=True)
                    last.then_inc(s_smp, 1)
                elif r == R_KT:
                    pe.wait_ge(s_kv, H * m + H)
                    if young(2):
                        pe.wait_ge(s_aot, m + 3)
                    for c in range(4):
                        last = transpose(b5[:, 128 * c:128 * c + 128], kv[:, 0, 2 * c:2 * c + 2, :].rearrange("t h d -> t (h d)"))
                    last.then_inc(s_ktp, 1)
                elif r == R_SC2 and not is_cls:
                    pe.wait_ge(s_kt, m + 1)
                    if young(2):
                        pe.wait_ge(s_pt, n + 3)
                        pe.wait_ge(s_h1, 2 * m + 6)
                    for e in range(2):
                        for c in range(4):
                            mm(wide[:, 512 * e + 128 * c:512 * e + 128 * c + 128], fq[64 * e:64 * e + 64, j % 2, c, :],
                               qk[64 * e:64 * e + 64, c, :], start=True, stop=True)
                    for c in range(4):
                        last = mm(b5[:, 2 * c:2 * c + 2], fq[:, j % 2, c, :], kcb[:, c, :], start=True, stop=True)
                    last.then_inc(s_sc2, 1)
                elif r == R_PV2 and not is_cls:
                    pe.wait_ge(s_pt2, n + 1)
                    pe.wait_ge(s_vf, m + 1)
                    if young(2):
                        pe.wait_ge(s_xt, 2 * m + 6)
                    for h in range(H):
                        last = mm(b5[:, D2 * h:D2 * h + D2], pt[:, h, :], vf[:, h, :], start=True, stop=True)
                    last.then_inc(s_pv2, 1)
                elif r == R_FOT:
                    if is_cls:
                        pe.wait_ge(s_vf, 1)
                    else:
                        pe.wait_ge(s_fo, 2 * n + 2)
                    src = vc if is_cls else fo
                    for c in range(4):
                        last = transpose(b5[:, 128 * c:128 * c + 128], src[:, 2 * c:2 * c + 2, :].rearrange("t h d -> t (h d)"))
                    last.then_inc(s_fop, 1)
                elif r == R_WO2:
                    pe.wait_ge(s_fot, m + 1)
                    if young(3):
                        pe.wait_ge(s_xt, 2 * m + 7)
                    for c in range(4):
                        last = mm(b5[:, 0:SIDE], aot[:, c, :], wo2s[:, c, :], start=(c == 0), stop=(c == 3))
                    last.then_inc(s_wo2, 1)

            def body(it, units, fno, tail):
                for u in range(units):
                    if fno:
                        unit(it, u)
                    for j, r, is_cls in tiles(it, u, tail):
                        tile(it, j, r, is_cls)
                    if fno:
                        unit_end(it, u)

            iterations(pe, body)

        @block.scalar
        def _(act):
            fn = nc.scalar.activation
            stage = tt[:, :, :, :, :].rearrange("k a b i c -> k (a b i c)")
            for c in range(4):
                act.wait_ge(s_wi, 16 * 4 * (c + 1))
                part = stage.rearrange("k (m r c) -> k m r c", r=2, c=CH)[:, :, 0, :]
                fn(part, part, ACT.Copy, scale=-1.0).then_inc(s_neg, 1)
            act.wait_ge(s_const, 16 * n_const[0])
            act.wait_ge(s_ws, 16 * (16 + 2 * LAYERS))

            def aligned(it, u, hb):
                s, i = divmod(u, GROUP)
                act.wait_ge(s_conv, U2 * it + 2 * u + hb + 1)
                if hb == 0:
                    v = u - 2
                    if v >= 0 and v < FOLDS:
                        act.wait_ge(s_fst, 3 * FOLDS * it + 3 * v + 3)
                        act.wait_ge(s_off[v % GROUP], 64 * LAYERS * it + 64 * (v // GROUP + 1))
                    elif v >= FOLDS or not first(it):
                        act.wait_ge(s_q1, 2 * GROUP * it + 2 * (v - FOLDS + 1) if v >= 0 else 2 * GROUP * it + 2 * (v + 1))
                dst = ha[:, u % 2, 16 * hb * PITCH:16 * (hb + 1) * PITCH].rearrange("k (y x) -> k y x", x=PITCH)[:, :, 0:BLK]
                fn(dst, cvb[hb][:, :].rearrange("k (y x) -> k y x", x=BLK), ACT.Identity,
                   bias=bias[:, s:s + 1]).then_inc(s_lin, 1)

            def turned(it, u, hb):
                s, i = divmod(u, GROUP)
                act.wait_ge(s_tr, 2 * FOLDS * it + 2 * u + hb + 1)
                if hb == 0 and i % 4 == 0:
                    if u == 0:
                        if not first(it):
                            act.wait_ge(s_rows, 16 * GROUP * it)
                    else:
                        act.wait_ge(s_fft, QUADS * it + 2 * s + i // 4)
                dst = tt[:, 4 * hb:4 * hb + 4, :, i % 4, :].rearrange("k a b c -> k (a b) c")
                fn(dst, tpb[:, :].rearrange("k (a c) -> k a c", c=CH), ACT.Copy).then_inc(s_tt, 1)

            def modes(it, s, q):
                act.wait_ge(s_fft, QUADS * it + 2 * s + q + 1)
                for i in range(4):
                    for ri in range(2):
                        src = b3[32 * i:32 * i + 32, 0:256].rearrange("k (q r m) -> k q r m", q=2, r=2)[:, :, ri, :]
                        dst = zz[32 * ri:32 * ri + 32, :, 4 * q + i].rearrange("k (q m) -> k q m", q=2)
                        last = fn(dst, src, ACT.Copy)
                last.then_inc(s_za, 1)

            def mixed(it, s, half):
                act.wait_ge(s_wchunk, CHUNKS * it + NWCH * (s - 1) + (NWCH // 2) * (half + 1))
                for p, bank in ((0, b3), (1, b4)):
                    dst = mx[64 * p:64 * p + 64, :, 64 * half:64 * half + 64].rearrange("k g m -> k m g")
                    last = fn(dst, bank[64 * p:64 * p + 64, :].rearrange("k (m g) -> k m g", g=GROUP), ACT.Copy)
                last.then_inc(s_mx, 1)

            def mode_rows(it, s, k):
                act.wait_ge(s_it, PI * it + 4 * (s - 1) + k + 1)
                if k:
                    act.wait_ge(s_v, 2 * PI * it + 8 * (s - 1) + 2 * k)
                src = b3[:, 0:256].rearrange("k (i a c) -> k i a c", i=2, a=4)
                fn(mt[:, :, :, :].rearrange("k a i c -> k i a c"), src, ACT.Copy).then_inc(s_mt, 1)

            def inv_y(it, s, k, half):
                g = 8 * (s - 1) + 2 * k + half
                act.wait_ge(s_v, 2 * PI * it + g + 1)
                if g or not first(it):
                    act.wait_ge(s_vs, 2 * PI * it + g)
                bank = b3 if half else b4
                fn(vt[:, :, :, :].rearrange("k a i c -> k (a i c)"), bank[:, 256:512], ACT.Copy).then_inc(s_vt, 1)

            def hidden(it, i, hb):
                g = 2 * GROUP * it + 2 * i + hb
                act.wait_ge(s_q1, g + 1)
                if i == 0 and hb == 0:
                    act.wait_ge(s_tr, 2 * FOLDS * it + 2 * FOLDS)
                if i:
                    act.wait_ge(s_q2, g - 1)
                fn(qh[:, 512 * hb:512 * hb + 512], tpb[:, :], ACT.Identity, bias=bias[:, 5:6]).then_inc(s_ql, 1)

            def token_rows(it, i, hb):
                act.wait_ge(s_q2, 2 * GROUP * it + 2 * i + hb + 1)
                if i and hb == 0:
                    act.wait_ge(s_rows, 16 * GROUP * it + 16 * i)
                for px in range(2):
                    dst = rr[:, 1024 * hb:1024 * hb + 1024].rearrange("p (n x) -> p n x", x=2)[:, :, px]
                    last = fn(dst, tpb[32 * px:32 * px + 2, :], ACT.Identity, bias=bias[32 * px:32 * px + 2, 6:7])
                last.then_inc(s_rr, 1)

            def unit(it, u):
                s, i = divmod(u, GROUP)
                if s >= 1 and i == 0:
                    mixed(it, s, 0)
                    mixed(it, s, 1)
                    mode_rows(it, s, 0)
                    inv_y(it, s, 0, 0)
                    inv_y(it, s, 0, 1)
                head = s == LAYERS and i >= 1
                if head:
                    hidden(it, i - 1, 0)
                aligned(it, u, 0)
                if s < LAYERS and i == 5:
                    modes(it, s, 0)
                if s >= 1 and i < 6:
                    if i % 2 == 0:
                        mode_rows(it, s, i // 2 + 1)
                    elif i < 5:
                        inv_y(it, s, i // 2 + 1, 1)
                if head:
                    token_rows(it, i - 1, 0)
                if s < LAYERS and i >= 1:
                    turned(it, u - 1, 0)
                if head:
                    hidden(it, i - 1, 1)
                aligned(it, u, 1)
                if s >= 1 and i < 6:
                    if i % 2 == 0:
                        inv_y(it, s, i // 2 + 1, 0)
                    elif i == 5:
                        inv_y(it, s, 3, 1)
                if head:
                    token_rows(it, i - 1, 1)
                if s < LAYERS and i >= 1:
                    turned(it, u - 1, 1)

            def unit_end(it, u):
                s, i = divmod(u, GROUP)
                if i == GROUP - 1 and s < LAYERS:
                    turned(it, u, 0)
                    turned(it, u, 1)
                    modes(it, s, 1)
                if i == GROUP - 1 and s == LAYERS:
                    for hb in range(2):
                        hidden(it, i, hb)
                        token_rows(it, i, hb)

            def copies(dst, src, done, scale=1.0):
                fn(dst, src, ACT.Copy, scale=scale).then_inc(done, 1)

            def tile(it, j, r, is_cls):
                m = tile_no(it, j)
                n = m - 1
                old = lambda k: older(it, j, k)
                young = lambda k: younger(it, j, k)
                if r in (R_LN1, R_WO1):
                    k = int(r == R_WO1)
                    act.wait_ge(s_ln, LN * m + 3 * k + 2)
                    fn(lnst[:, k, 8:9], lnst[:, k, 7:8], ACT.Sqrt, bias=bias[:, 7:8]).then_inc(s_sd, 1)
                elif r in (R_XT1, R_XT2):
                    k = int(r == R_XT2)
                    act.wait_ge(s_xtp, 2 * m + k + 1)
                    if k:
                        act.wait_ge(s_qkp, m + 1)
                    elif not is_cls:
                        act.wait_ge(s_qpp, m)
                    copies(xnt[0:SIDE, :], b5[0:SIDE, 0:128], s_xt)
                elif r == R_QKV:
                    act.wait_ge(s_qkp, m + 1)
                    src = wide[:, 256:512].rearrange("k (c t) -> k c t", c=2)
                    if is_cls:
                        for a in range(4):
                            last = fn(k0b[32 * a:32 * a + 32, :, a], src[32 * a:32 * a + 32, :, 0], ACT.Copy)
                    else:
                        if old(1):
                            act.wait_ge(s_scp, n)
                        fn(qt[:, :, :].rearrange("k c t -> k (c t)"), wide[:, 0:256], ACT.Copy, scale=float(D1) ** -0.5)
                        for a in range(4):
                            last = fn(kb[32 * a:32 * a + 32, :, a, :], src[32 * a:32 * a + 32, :, :], ACT.Copy)
                    last.then_inc(s_qka, 1)
                elif r in (R_PT1, R_PT2) and not is_cls:
                    one = r == R_PT1
                    act.wait_ge(s_sm1 if one else s_sm2, SM * n + 3)
                    fn(ee[:, :, :].rearrange("t h s -> t (h s)"), ee[:, :, :].rearrange("t h s -> t (h s)"), ACT.Exp)\
                        .then_inc(s_ex1 if one else s_ex2, 1)
                    act.wait_ge(s_ptp if one else s_pt2p, n + 1)
                    if one and old(3):
                        act.wait_ge(s_pv2, n - 2)
                    if not one and young(2):
                        act.wait_ge(s_pvp, n + 3)
                    for c in range(2):
                        last = fn(pt[:, 4 * c:4 * c + 4, :].rearrange("s h t -> s (h t)"), wide[:, 512 * c:512 * c + 512], ACT.Copy)
                    last.then_inc(s_pt if one else s_pt2, 1)
                elif r == R_AOT:
                    act.wait_ge(s_aop, m + 1)
                    if old(3):
                        act.wait_ge(s_wo2, m - 2)
                    copies(aot[:, 0:2, :].rearrange("k c t -> k (c t)"), b5[:, 0:256], s_aot)
                elif r == R_QPK:
                    act.wait_ge(s_qpp, m + 1)
                    if old(2):
                        act.wait_ge(s_sc2, n - 1)
                    copies(qk[:, :, :].rearrange("k c t -> k (c t)"), wide[:, 0:512], s_qp)
                    copies(fq[:, j % 2, :, :].rearrange("k c t -> k (c t)"), wide[:, 512:1024], s_fq, float(D2) ** -0.5)
                elif r == R_SIM:
                    act.wait_ge(s_smp, m + 1)
                    if not is_cls:
                        act.wait_ge(s_dst, DEC * m)
                    if old(2):
                        act.wait_ge(s_pt2p, n - 1)
                        act.wait_ge(s_sm2, SM * (n - 2) + 6)
                    for c in range(2):
                        last = fn(sim[:, 8 * c:8 * c + 8, :].rearrange("t g k -> t (g k)"), wide[:, 512 * c:512 * c + 512], ACT.Copy)
                    last.then_inc(s_sim, 1)
                elif r == R_CAND:
                    act.wait_ge(s_pws, PW * m + 1)
                    w = pwt[:, j % 2, :, :].rearrange("t h k -> t (h k)")
                    fn(w, w, ACT.Exp).then_inc(s_pwe, 1)
                elif r == R_KT:
                    act.wait_ge(s_ktp, m + 1)
                    if is_cls:
                        for e in range(2):
                            last = fn(kcb[64 * e:64 * e + 64, :, e], b5[64 * e:64 * e + 64, :]
                                      .rearrange("k (c t) -> k c t", c=4)[:, :, 0], ACT.Copy)
                        last.then_inc(s_kt, 1)
                    else:
                        if young(1):
                            act.wait_ge(s_smp, m + 2)
                        copies(qk[:, :, :].rearrange("k c t -> k (c t)"), b5[:, :], s_kt)
                elif r == R_FOT:
                    act.wait_ge(s_fop, m + 1)
                    if young(2):
                        act.wait_ge(s_wop, m + 3)
                    copies(aot[:, :, :].rearrange("k c t -> k (c t)"), b5[:, :], s_fot)

            def body(it, units, fno, tail):
                for u in range(units):
                    if fno:
                        unit(it, u)
                    for j, r, is_cls in tiles(it, u, tail):
                        tile(it, j, r, is_cls)
                    if fno:
                        unit_end(it, u)

            iterations(act, body)

        @block.vector
        def _(dve):
            v = nc.vector
            dve.wait_ge(s_const, 16 * n_const[0])

            def inv_y(it, s, k, half):
                dve.wait_ge(s_vt, 2 * PI * it + 8 * (s - 1) + 2 * k + half + 1)
                bank = b3 if half else b4
                even = bank[:, 0:256].rearrange("k (a i c) -> k a i c", a=4, i=2)
                for low, op in ((0, ALU.add), (4, ALU.subtract)):
                    c0 = low + 2 * half
                    dst = vs[:, k % 2, :, c0:c0 + 2, :, :].rearrange("k i a b c -> k (a b) i c")
                    last = v.tensor_tensor(dst, even, vt[:, :, :, :], op)
                last.then_inc(s_vs, 1)

            def folds(it, u):
                image_ready(dve, it, u)
                if u == 0 and not first(it):
                    dve.wait_ge(s_q2, 2 * GROUP * it)
                img = ha[:, u % 2, :].rearrange("k (y x) -> k y x", x=PITCH)
                base = 3 * FOLDS * it + 3 * u
                if u or not first(it):
                    dve.wait_ge(s_fold, FOLDS * it + u)
                for p, op in ((0, ALU.add), (1, ALU.subtract)):
                    if p:
                        dve.wait_ge(s_fst, base + 2)
                    v.tensor_tensor(fold1[:, :, :], img[:, 0:16, 0:BLK], img[:, 16:32, 0:BLK], op).then_inc(s_fst, 1)
                    dve.wait_ge(s_fst, base + 2 * p + 1)
                    if p == 0 and (u or not first(it)):
                        dve.wait_ge(s_tr, 2 * FOLDS * it + 2 * u)
                    for q, op2 in ((0, ALU.add), (1, ALU.subtract)):
                        last = v.tensor_tensor(fold[:, p, q, :, :], fold1[:, :, 0:16], fold1[:, :, 16:32], op2)
                    if p == 0:
                        last.then_inc(s_fst, 1)
                last.then_inc(s_fold, 1)

            def modes(it, s, q):
                dve.wait_ge(s_fft, QUADS * it + 2 * s + q + 1)
                for i in range(4):
                    for ri in range(2):
                        src = b4[32 * i:32 * i + 32, 0:256].rearrange("k (q r m) -> k q r m", q=2, r=2)[:, :, ri, :]
                        dst = zz[64 + 32 * ri:96 + 32 * ri, :, 4 * q + i].rearrange("k (q m) -> k q m", q=2)
                        last = v.tensor_copy(dst, src)
                last.then_inc(s_zd, 1)

            def rectified(it, u, hb):
                dve.wait_ge(s_lin, U2 * it + 2 * u + hb + 1)
                img = ha[:, u % 2, 16 * hb * PITCH:16 * (hb + 1) * PITCH].rearrange("k (y x) -> k y x", x=PITCH)[:, :, 0:BLK]
                v.scalar_tensor_tensor(img, img, SLOPE, img, ALU.mult, ALU.max).then_inc(s_act, 1)

            def hidden(it, i, hb):
                dve.wait_ge(s_ql, 2 * GROUP * it + 2 * i + hb + 1)
                part = qh[:, 512 * hb:512 * hb + 512]
                v.scalar_tensor_tensor(part, part, SLOPE, part, ALU.mult, ALU.max).then_inc(s_qh, 1)

            def unit(it, u):
                s, i = divmod(u, GROUP)
                if s >= 1 and i == 0:
                    inv_y(it, s, 0, 0)
                    inv_y(it, s, 0, 1)
                if s == LAYERS and i >= 1:
                    hidden(it, i - 1, 0)
                if s >= 1:
                    rectified(it, u, 0)
                if s < LAYERS and i == 5:
                    modes(it, s, 0)
                if s >= 1 and i in (1, 3):
                    inv_y(it, s, i // 2 + 1, 1)
                if s == LAYERS and i >= 1:
                    hidden(it, i - 1, 1)
                if s >= 1:
                    rectified(it, u, 1)
                if s >= 1 and i < 6 and i % 2 == 0:
                    inv_y(it, s, i // 2 + 1, 0)
                if s >= 1 and i == 5:
                    inv_y(it, s, 3, 1)
                if s < LAYERS:
                    folds(it, u)

            def unit_end(it, u):
                s, i = divmod(u, GROUP)
                if i == GROUP - 1 and s < LAYERS:
                    modes(it, s, 1)
                if i == GROUP - 1 and s == LAYERS:
                    for hb in range(2):
                        hidden(it, i, hb)

            def layer_stats(m, k, src, is_cls):
                base = LN * m + 3 * k
                if not is_cls:
                    dve.wait_ge(s_ln, LN * m)
                    dve.wait_ge(s_xn, 2 * m)
                v.bn_stats(lnst[:, k, 0:6], src).then_inc(s_ln, 1)
                dve.wait_ge(s_ln, base + 1)
                held(dve, "dve")
                v.bn_aggr(lnst[:, k, 6:8], lnst[:, k, 0:6]).then_inc(s_ln, 1)

            def normed(m, k, src, is_cls):
                dve.wait_ge(s_sd, 2 * m + k + 1)
                v.reciprocal(lnst[:, k, 9:10], lnst[:, k, 8:9]).then_inc(s_ln, 1)
                dve.wait_ge(s_ln, LN * m + 3 * k + 3)
                if k or not is_cls:
                    dve.wait_ge(s_xtp, 2 * m + k)
                v.tensor_scalar(xn[:, :], src, lnst[:, k, 6:7], lnst[:, k, 9:10], ALU.subtract, ALU.mult).then_inc(s_xn, 1)

            def shares(a, n, ex, steps):
                dve.wait_ge(ex, n + 1)
                v.tensor_reduce(smx[:, a, 1, :], ee[:, :, :], AX.X, ALU.add).then_inc(steps, 1)
                dve.wait_ge(steps, SM * n + 4)
                v.reciprocal(smx[:, a, 2, :], smx[:, a, 1, :]).then_inc(steps, 1)
                dve.wait_ge(steps, SM * n + 5)
                v.tensor_tensor(smx[:, a, 3, :], ee[:, :, 128], smx[:, a, 2, :], ALU.mult).then_inc(steps, 1)

            def shift(it, a, n, steps):
                if not (static(it) and n == 0):
                    dve.wait_ge(s_fo if a else s_ao, 2 * n if a else 3 * n)
                dve.wait_ge(steps, SM * n + 1)
                v.tensor_reduce(smx[:, a, 0, :], ee[:, :, :], AX.X, ALU.max).then_inc(steps, 1)
                dve.wait_ge(steps, SM * n + 2)
                v.tensor_tensor(ee[:, :, :], ee[:, :, :], smx[:, a, 0, :].unsqueeze(2).to_broadcast([128, H, 129]),
                                ALU.subtract).then_inc(steps, 1)

            def tile(it, j, r, is_cls):
                m = tile_no(it, j)
                n = m - 1
                old = lambda k: older(it, j, k)
                young = lambda k: younger(it, j, k)
                if r == R_LN1:
                    if not is_cls:
                        dve.wait_ge(s_ht[j % PAIRS], 16 * it)
                    layer_stats(m, 0, ht[:, j % PAIRS, :], is_cls)
                elif r == R_XT1:
                    normed(m, 0, ht[:, j % PAIRS, :], is_cls)
                elif r == R_QKV:
                    dve.wait_ge(s_qkp, m + 1)
                    v.tensor_copy((v0 if is_cls else vv)[:, :, :].rearrange("t h d -> t (h d)"), wide[:, 512:768]).then_inc(s_qkd, 1)
                elif r == R_SC1 and not is_cls:
                    dve.wait_ge(s_scp, n + 1)
                    dve.wait_ge(s_top, TOPS * m)
                    for h in range(H):
                        v.scalar_tensor_tensor(ee[:, h, 0:128], rel[:, :], 0.5 ** (h + 1), wide[:, 128 * h:128 * h + 128],
                                               ALU.mult, ALU.add)
                    v.tensor_tensor(ee[:, :, 128], b5[:, 0:H], relcls[:, :], ALU.add).then_inc(s_sm1, 1)
                    shift(it, 0, n, s_sm1)
                elif r == R_PT1 and not is_cls:
                    shares(0, n, s_ex1, s_sm1)
                elif r == R_PV1 and not is_cls:
                    dve.wait_ge(s_pvp, n + 1)
                    dve.wait_ge(s_sm1, SM * n + 6)
                    wide1 = [128, H, D1]
                    dve.wait_ge(s_cst, CS * m)
                    if old(3):
                        dve.wait_ge(s_fo, 2 * n - 4)
                    v.tensor_tensor(atmp, v0[:, :, :], smx[:, 0, 3, :].unsqueeze(2).to_broadcast(wide1), ALU.mult).then_inc(s_ao, 1)
                    if old(3):
                        dve.wait_ge(s_fop, m - 2)
                    v.tensor_tensor(ao, b5[:, 0:256].rearrange("t (h d) -> t h d", h=H),
                                    smx[:, 0, 2, :].unsqueeze(2).to_broadcast(wide1), ALU.mult).then_inc(s_ao, 1)
                    dve.wait_ge(s_ao, 3 * n + 2)
                    v.tensor_tensor(ao, ao, atmp, ALU.add).then_inc(s_ao, 1)
                elif r == R_WO1:
                    slot = j % PAIRS
                    if not static(it) or m == 1 or m >= 5:
                        dve.wait_ge(s_ob, 1 if static(it) and m == 1 else m - 3)
                    v.tensor_tensor(h1[:, slot, :], ht[:, slot, :], bob[:, :], ALU.add).then_inc(s_h1, 1)
                    dve.wait_ge(s_wop, m + 1)
                    dve.wait_ge(s_h1, 2 * m + 1)
                    v.tensor_tensor(h1[:, slot, :], h1[:, slot, :], b5[:, 0:SIDE], ALU.add).then_inc(s_h1, 1)
                    dve.wait_ge(s_h1, 2 * m + 2)
                    layer_stats(m, 1, h1[:, slot, :], is_cls)
                elif r == R_XT2:
                    normed(m, 1, h1[:, j % PAIRS, :], is_cls)
                elif r in (R_TOP0, R_TOP1):
                    p = int(r == R_TOP1)
                    base = TOPS * m + 4 * p
                    if p or not is_cls:
                        dve.wait_ge(s_top, base)
                    if p == 0 and not is_cls:
                        dve.wait_ge(s_cst, CS * m)
                        dve.wait_ge(s_ao, 3 * n + 3)
                        if old(2):
                            dve.wait_ge(s_fo, 2 * n - 2)
                    dve.wait_ge(s_sim, m + 1)
                    held(dve, "dve")
                    for h in range(H):
                        last = v.max(tv[:, p, h, 0:8], sim[:, H * p + h, :])
                    last.then_inc(s_top, 1)
                    dve.wait_ge(s_top, base + 1)
                    held(dve, "dve")
                    for h in range(H):
                        v.max_index(ti[:, p, h, 0:8], tv[:, p, h, 0:8], sim[:, H * p + h, :])
                        last = v.match_replace(rest[:, h, :], tv[:, p, h, 0:8], sim[:, H * p + h, :], LOW)
                    last.then_inc(s_top, 1)
                    dve.wait_ge(s_top, base + 2)
                    held(dve, "dve")
                    for h in range(H):
                        last = v.max(tv[:, p, h, 8:16], rest[:, h, :])
                    last.then_inc(s_top, 1)
                    dve.wait_ge(s_top, base + 3)
                    held(dve, "dve")
                    for h in range(H):
                        last = v.max_index(ti[:, p, h, 8:16], tv[:, p, h, 8:16], rest[:, h, :])
                    last.then_inc(s_top, 1)
                elif r == R_CAND:
                    base = CS * m
                    dve.wait_ge(s_top, TOPS * m + 8)
                    if not is_cls:
                        dve.wait_ge(s_dst, DEC * m)
                        dve.wait_ge(s_pws, PW * m)
                        dve.wait_ge(s_aop, m + 1)
                        if not (static(it) and m < 2):
                            dve.wait_ge(s_mul, 2 * H * (m - 1))
                    v.tensor_tensor(tf[:, 0, :, :], ti[:, 0, :, :], headoff[:, :].unsqueeze(2).to_broadcast([128, H, TOP]), ALU.add)
                    v.tensor_scalar(tf[:, 1, :, :], ti[:, 1, :, :], float(KEYS), None, ALU.mult).then_inc(s_cst, 1)
                    dve.wait_ge(s_cst, base + 1)
                    if old(2):
                        dve.wait_ge(s_fop, m - 1)
                    at = 0
                    for a, na, nb in CAND:
                        for dst, src in ((cs, tv), (ci_, tf)):
                            last = v.tensor_tensor(
                                dst[:, :, at:at + na * nb].rearrange("t h (a b) -> t h a b", b=nb),
                                src[:, 0, :, a:a + na].unsqueeze(3).to_broadcast([128, H, na, nb]),
                                src[:, 1, :, 0:nb].unsqueeze(2).to_broadcast([128, H, na, nb]), ALU.add)
                        at += na * nb
                    last.then_inc(s_cst, 1)
                    dve.wait_ge(s_cst, base + 2)
                    held(dve, "dve")
                    for h in range(H):
                        last = v.max(fv[:, h, 0:8], cs[:, h, :])
                    last.then_inc(s_cst, 1)
                    dve.wait_ge(s_cst, base + 3)
                    held(dve, "dve")
                    for h in range(H):
                        v.max_index(fp[:, h, 0:8], fv[:, h, 0:8], cs[:, h, :])
                        last = v.match_replace(crest[:, h, :], fv[:, h, 0:8], cs[:, h, :], LOW)
                    last.then_inc(s_cst, 1)
                    dve.wait_ge(s_cst, base + 4)
                    held(dve, "dve")
                    for h in range(H):
                        last = v.max(fv[:, h, 8:16], crest[:, h, :])
                    last.then_inc(s_cst, 1)
                    dve.wait_ge(s_cst, base + 5)
                    v.tensor_tensor(pwt[:, j % 2, :, :], fv[:, :, :], fv[:, :, 0:1].to_broadcast([128, H, TOP]),
                                    ALU.subtract).then_inc(s_pws, 1)
                    for h in range(H):
                        last = v.max_index(fp[:, h, 8:16], fv[:, h, 8:16], crest[:, h, :])
                    last.then_inc(s_cst, 3)
                elif r == R_SOFT:
                    dve.wait_ge(s_pwe, m + 1)
                    w = pwt[:, j % 2, :, :]
                    v.tensor_reduce(psm[:, 0, :], w, AX.X, ALU.add).then_inc(s_pws, 1)
                    dve.wait_ge(s_pws, PW * m + 2)
                    v.reciprocal(psm[:, 1, :], psm[:, 0, :]).then_inc(s_pws, 1)
                    dve.wait_ge(s_pws, PW * m + 3)
                    v.tensor_tensor(w, w, psm[:, 1, :].unsqueeze(2).to_broadcast([128, H, TOP]), ALU.mult).then_inc(s_pws, 1)
                elif r in R_DEC:
                    group = list(R_DEC).index(r)
                    h0, h1_ = R_DEC[r]
                    if group == 0:
                        dve.wait_ge(s_cst, CS * m + 8)
                        if young(1):
                            dve.wait_ge(s_ptp, n + 2)
                            dve.wait_ge(s_sm1, SM * n + 12)
                    for h in range(h0, h1_):
                        base = DEC * m + 3 * h + group
                        full = [128, TOP, NCAND]
                        if not (first(it) and h == 0):
                            dve.wait_ge(s_dst, base)
                        v.tensor_tensor(hot, fp[:, h, :].unsqueeze(2).to_broadcast(full), iota[:, :].unsqueeze(1).to_broadcast(full),
                                        ALU.is_equal).then_inc(s_dst, 1)
                        dve.wait_ge(s_dst, base + 1)
                        v.tensor_tensor(hot, hot, ci_[:, h, :].unsqueeze(1).to_broadcast(full), ALU.mult).then_inc(s_dst, 1)
                        dve.wait_ge(s_dst, base + 2)
                        v.tensor_reduce(fx[:, h, :], hot, AX.X, ALU.add).then_inc(s_dst, 1)
                    dve.wait_ge(s_dst, DEC * m + 3 * h1_ + group)
                    v.tensor_copy(ix[:, j % 2, h0:h1_, :], fx[:, h0:h1_, :]).then_inc(s_dst, 1)
                elif r in R_SUM:
                    for q in range(*R_SUM[r]):
                        h, half = divmod(q, 2)
                        if q == 0:
                            dve.wait_ge(s_pws, PW * m + 4)
                            if not is_cls:
                                dve.wait_ge(s_ktp, m)
                                dve.wait_ge(s_vf, m)
                        slot = q % GRING
                        dve.wait_ge(s_g[q], 16 * HALF * (m + 1))
                        rows8 = gg[:, slot, :, :]
                        v.tensor_tensor(rows8, rows8, pwt[:, j % 2, h, HALF * half:HALF * half + HALF].unsqueeze(2)
                                        .to_broadcast([128, HALF, 128]), ALU.mult).then_inc(s_mul, 1)
                        dve.wait_ge(s_mul, 2 * H * m + q + 1)
                        if half and not (first(it) and h == 0):
                            dve.wait_ge(s_kv, H * m + h)
                        v.tensor_reduce(kvh[:, :, :] if half else kv[:, :, h, :],
                                        rows8.rearrange("t k (w d) -> t w d k", w=2), AX.X, ALU.add)\
                            .then_inc(s_red, 1)
                        if half:
                            dve.wait_ge(s_red, 2 * H * m + q + 1)
                            v.tensor_tensor(kv[:, :, h, :], kv[:, :, h, :], kvh[:, :, :], ALU.add).then_inc(s_kv, 1)
                elif r == R_KT:
                    dve.wait_ge(s_kv, H * m + H)
                    if old(1):
                        dve.wait_ge(s_pv2, n)
                    v.tensor_copy((vc if is_cls else vf)[:, :, :], kv[:, 1, :, :]).then_inc(s_vf, 1)
                elif r == R_SC2 and not is_cls:
                    dve.wait_ge(s_sc2, n + 1)
                    dve.wait_ge(s_dst, DEC * m + DEC * (2 if young(1) else 1))
                    for e in range(2):
                        v.tensor_tensor(ee[:, :, 0:128].rearrange("t (c e) s -> t c e s", e=2)[:, :, e, :],
                                        wide[:, 512 * e:512 * e + 512].rearrange("t (c s) -> t c s", c=4),
                                        mask[:, :].unsqueeze(1).to_broadcast([128, 4, 128]), ALU.add)
                    v.tensor_copy(ee[:, :, 128], b5[:, 0:H]).then_inc(s_sm2, 1)
                    shift(it, 1, n, s_sm2)
                elif r == R_PT2 and not is_cls:
                    shares(1, n, s_ex2, s_sm2)
                elif r == R_PV2 and not is_cls:
                    dve.wait_ge(s_pv2, n + 1)
                    dve.wait_ge(s_sm2, SM * n + 6)
                    full = [128, H, D2]
                    if young(1):
                        dve.wait_ge(s_cst, CS * m + 2 * CS)
                    if young(2):
                        dve.wait_ge(s_ao, 3 * n + 9)
                    v.tensor_tensor(ftmp[:, :, :], vc[:, :, :], smx[:, 1, 3, :].unsqueeze(2).to_broadcast(full), ALU.mult)
                    if young(2):
                        dve.wait_ge(s_aop, m + 3)
                    v.tensor_tensor(fo[:, :, :], b5[:, :].rearrange("t (h d) -> t h d", h=H),
                                    smx[:, 1, 2, :].unsqueeze(2).to_broadcast(full), ALU.mult).then_inc(s_fo, 1)
                    dve.wait_ge(s_fo, 2 * n + 1)
                    v.tensor_tensor(fo[:, :, :], fo[:, :, :], ftmp[:, :, :], ALU.add).then_inc(s_fo, 1)
                elif r == R_WO2:
                    dve.wait_ge(s_wo2, m + 1)
                    if not is_cls:
                        e = j % 2
                        stored = 32 * (2 * (it - 1) + j // 2) + 16 * (1 - e)
                        if not static(it) or stored > 0:
                            dve.wait_ge(s_out[e], stored)
                    v.tensor_tensor(ob[:, j % 2, :], h1[:, j % PAIRS, :], b5[:, 0:SIDE], ALU.add).then_inc(s_ob, 1)

            def body(it, units, fno, tail):
                for u in range(units):
                    if fno:
                        unit(it, u)
                    for j, r, is_cls in tiles(it, u, tail):
                        tile(it, j, r, is_cls)
                    if fno:
                        unit_end(it, u)

            iterations(dve, body)


def constants():
    f = np.float64
    ft = np.zeros((128, 32, 128), f)
    i1 = np.zeros((128, 32, 128), f)
    y8, x16 = np.divmod(np.arange(128), 16)
    a, b = np.divmod(np.arange(64), 8)
    for p in range(2):
        for q in range(2):
            for j in range(2):
                for px in range(2):
                    for py in range(2):
                        y, x = 2 * (8 * j + y8) + py, 2 * x16 + px
                        th = 2 * np.pi / SIDE * (np.outer(y, 2 * a + p) + np.outer(x, 2 * b + q))
                        ft[:, 8 * (2 * p + q) + 4 * j + 2 * px + py] = np.concatenate([np.cos(th), -np.sin(th)], 1)
    qi, rem = np.divmod(np.arange(128), 64)
    ai, bi = np.divmod(rem, 8)
    ky = 2 * bi + qi
    y4, rest = np.divmod(np.arange(128), 32)
    kyo, ro = np.divmod(rest, 2)
    same = ky[:, None] == kyo[None, :]
    for p in range(2):
        kx = 2 * ai + p
        for ri in range(2):
            for c in range(4):
                for py in range(2):
                    y = 2 * (4 * c + y4) + py
                    th = 2 * np.pi / SIDE * np.outer(kx, y)
                    if ri == 0:
                        w = np.where(ro[None, :] == 0, np.cos(th), np.sin(th))
                    else:
                        w = np.where(ro[None, :] == 0, -np.sin(th), np.cos(th))
                    i1[:, 8 * (2 * p + ri) + 2 * c + py] = w * same / SIDE
    i2 = np.zeros((128, 2, 128), f)
    yo, xo = np.divmod(np.arange(128), BLK)
    for px in range(2):
        th = 2 * np.pi / SIDE * np.outer(kyo, 2 * xo + px)
        w = np.where(ro[:, None] == 0, np.cos(th), -np.sin(th)) * np.where(kyo[:, None] == 0, 1, 2) / SIDE
        i2[:, px] = w * (y4[:, None] == yo[None, :])
    t = np.arange(128)
    seen = (t[:, None] // SIDE == t[None, :] // SIDE) & (t[None, :] <= t[:, None])
    rel = np.stack([np.where(seen, t[None, :] - t[:, None], NEG), np.where(seen, 0, NEG)])
    relcls = -(t[:, None] % SIDE + 1) * 0.5 ** (np.arange(H) + 1)[None, :]
    cst = {"ft_c": ft, "i1_c": i1, "i2_c": i2, "ident_c": np.eye(128), "rel_c": rel, "relcls_c": relcls,
           "iota_c": np.tile(np.arange(NCAND), (128, 1)), "head_c": np.tile(np.arange(H) * KEYS * KEYS, (128, 1))}
    return {k: np.ascontiguousarray(w.astype(np.float32)) for k, w in cst.items()}


def by_class(w):
    n = w.shape[0]
    w = w.reshape(n, CH, CH, 8, 2, 8, 2).transpose(0, 4, 1, 6, 3, 5, 2)
    return w.reshape(n, 2, CH, HM, CH)


def kernel(**inputs):
    import concourse.bacc as bacc
    from concourse.bass_utils import run_bass_kernel_spmd

    g = {k: np.asarray(w) for k, w in inputs.items()}
    x = g["x"].reshape(IMGS, BLK, 2, BLK, 2, 3).transpose(0, 4, 2, 5, 1, 3).reshape(IMGS, 12, BLK * BLK)
    grid = g["L0_tok_input_grid"].reshape(BLK, 2, BLK, 2, 2).transpose(3, 1, 4, 0, 2).reshape(8, BLK * BLK)
    wr_, wi_ = by_class(g["L0_tok_spec_wr"]), by_class(g["L0_tok_spec_wi"])
    wl = np.stack([np.stack([wr_, wi_], 4), np.stack([wi_, wr_], 4)], 2).reshape(LAYERS, 128, HM * 2 * CH)
    arrays = {
        "x12": x, "grid8": grid, "pw": g["L0_tok_P_w"], "pb": g["L0_tok_P_b"], "wl": wl,
        "cwt": g["L0_tok_conv_w"].transpose(3, 4, 2, 0, 1), "cb": g["L0_tok_conv_b"],
        "q1w": g["L0_tok_Q1_w"], "q1b": g["L0_tok_Q1_b"], "q2w": g["L0_tok_Q2_w"], "q2b": g["L0_tok_Q2_b"],
        "cls": g["cls_tok"], "wq": g["L0_attn_Wq"], "wk": g["L0_attn_Wk"], "wv": g["L0_attn_Wv"],
        "wo": g["L0_attn_Wo"], "bo": g["L0_attn_bo"], "wqpk": g["L0_ffn_Wq_pk"],
        "keyst": g["L0_ffn_pk_keys"].transpose(0, 2, 3, 1), "wq2": g["L0_ffn_Wq"],
        "table": np.concatenate([g["L0_ffn_keys_table"], g["L0_ffn_values_table"]], 1), "wo2": g["L0_ffn_Wo"],
    } | constants()

    nc = bacc.Bacc("TRN2", target_bir_lowering=False, num_devices=1)
    nc.disable_value_cache = True
    maps, args = {}, {}
    for name, a in arrays.items():
        a = np.ascontiguousarray(a)
        maps[f"in_{name}"] = a
        args[name] = nc.dram_tensor(f"in_{name}", a.shape, mybir.dt.from_np(a.dtype), kind="ExternalInput").ap()
    args["out"] = nc.dram_tensor("out_tokens", (IMGS, SIDE + 1, SIDE), F32, kind="ExternalOutput").ap()
    tower_kernel(nc, **args)
    r = run_bass_kernel_spmd(nc, [maps], core_ids=[0])
    return r.results[0]["out_tokens"]
```

```python
from contextlib import ExitStack

import numpy as np

import concourse.bass as bass
from concourse import mybir

F32 = mybir.dt.float32
U32 = mybir.dt.uint32
ALU = mybir.AluOpType
ACT = mybir.ActivationFunctionType
AX = mybir.AxisListType

IMGS = 128
SIDE = 64
CH = 32
LAYERS = 4
MODES = 16
GROUP = 8
GROUPS = IMGS // GROUP
PAIRS = GROUP // 2
STAGES = LAYERS + 1
UNITS = STAGES * GROUP
BLK = SIDE // 2
PITCH = BLK + 1
HA_LEN = BLK * PITCH
OFF_LEN = PITCH * PITCH + 1
HM = 128
WCH = 16
NWCH = HM // WCH
WRING = 4
H = 8
D1 = 32
D2 = 64
KEYS = 64
TOP = 16
ROWS = H * KEYS * KEYS
SPAN = 10
HALF = TOP // 2
GRING = 3
EPS = 1e-5
SLOPE = 0.01
NEG = -1e30
LOW = -3e38
CAND = [(0, 1, 16), (1, 1, 8), (2, 1, 5), (3, 1, 4), (4, 1, 3), (5, 3, 2), (8, 8, 1)]
NCAND = sum(n * b for _, n, b in CAND)

R_LN1, R_XT1, R_QKV, R_SC1, R_PT1, R_PV1, R_AOT, R_WO1, R_XT2, R_QPK = range(10)
R_SIM, R_TOP0, R_TOP1, R_CAND, R_SOFT = range(10, 15)
R_DEC = {15: (0, 2), 16: (2, 5), 17: (5, 8)}
R_SUM = {18: (0, 2), 19: (2, 5), 20: (5, 7), 21: (7, 9), 22: (9, 11), 24: (11, 14), 25: (14, 15), 26: (15, 16)}
R_KT, R_SC2, R_PT2, R_PV2, R_FOT, R_WO2, R_OUT = range(27, 34)


def tower_kernel(nc, x12, grid8, pw, pb, wl, cwt, cb, q1w, q1b, q2w, q2b, cls, wq, wk, wv, wo,
                 bo, wqpk, keyst, wq2, table, wo2, ft_c, i1_c, i2_c, ident_c, rel_c, relcls_c,
                 iota_c, head_c, out):
    ctx = ExitStack()
    with ctx:
        def sb(name, shape, dt=F32):
            return ctx.enter_context(nc.sbuf_tensor(name, shape, dt))

        def pb_(name):
            return ctx.enter_context(nc.psum_tensor(name, [128, 512], F32))

        def sem(name):
            return ctx.enter_context(nc.semaphore(name))

        wmix = nc.dram_tensor("wmix", (LAYERS, 128, HM * 2 * CH), F32, kind="Internal").ap()
        turned = nc.dram_tensor("turned", (HM, 2 * GROUP, 2 * CH), F32, kind="Internal").ap()
        rows = nc.dram_tensor("rows", (IMGS * SIDE, SIDE), F32, kind="Internal").ap()

        off = sb("off", [128, GROUP, OFF_LEN])
        ha = sb("ha", [128, 2, HA_LEN])
        fold1 = sb("fold1", [128, 16, BLK])
        fold = sb("fold", [128, 2, 2, 16, 16])
        qh = fold[:, :, :, :, :].rearrange("c p q y x -> c (p q y x)")
        tt = sb("tt", [128, 8, 4, 4, CH])
        zz = sb("zz", [128, HM, 2, GROUP])
        mo = tt[:, :, :, :, :].rearrange("k a b i c -> k (a b i c)")[:, 2048:4096]
        mt = sb("mt", [128, 2, GROUP, 2, CH])
        vt = sb("vt", [128, 2, 4, CH])
        vs = sb("vs", [128, 2, 4, 8, 2, CH])
        wr = vs[:, :, :, :, :, :].rearrange("k s i a b c -> k (s i a b c)").rearrange("k (r w) -> k r w", r=WRING)
        ft = sb("ft", [128, 4 * 8, 128])
        i1 = sb("i1", [128, 32, 128])
        i2 = sb("i2", [128, 2, 128])
        ident = sb("ident", [128, 128])
        cw = sb("cw", [128, LAYERS, 4, 128])
        lw = sb("lw", [128, 128])
        q1 = sb("q1", [128, 128])
        q2 = sb("q2", [128, 34])
        bias = sb("bias", [128, 8])
        xl = vs[:, 0, :, :, :, :].rearrange("k i a b c -> k (i a b c)").rearrange("k (s n) -> k s n", s=2)
        rr = tt[0:2, :, :, :, :].rearrange("k a b i c -> k (a b i c)")[:, 0:2048]

        ht = sb("ht", [128, 4, SIDE])
        h1 = sb("h1", [128, 4, SIDE])
        lnst = sb("lnst", [128, 2, 6 + 4])
        xn = sb("xn", [128, SIDE])
        xnt = sb("xnt", [128, 128])
        qt = sb("qt", [128, 2, 128])
        kb = sb("kb", [128, 2, 4, 128])
        vv = sb("vv", [128, H, D1])
        ee = sb("ee", [128, H, 129])
        pt = sb("pt", [128, H, 128])
        fo = sb("fo", [128, H, D2])
        ao = fo[:, :, :].rearrange("t h d -> t (h d)")[:, 0:H * D1].rearrange("t (h d) -> t h d", h=H)
        rest = sb("rest", [128, H, KEYS])
        ftmp = rest
        atmp = ftmp[:, :, :].rearrange("t h d -> t (h d)")[:, 0:H * D1].rearrange("t (h d) -> t h d", h=H)
        aot = sb("aot", [128, 4, 128])
        smx = sb("smx", [128, 2, 4, H])
        qk = sb("qk", [128, 4, 128])
        fq = sb("fq", [128, 2, 4, 128])
        sim = ee[:, :, :].rearrange("t h s -> t (h s)")[:, 0:1024].rearrange("t (g k) -> t g k", k=KEYS)
        hot = ee[:, :, :].rearrange("t h s -> t (h s)")[:, 0:TOP * NCAND].rearrange("t (k c) -> t k c", k=TOP)
        tv = sb("tv", [128, 2, H, TOP])
        ti = sb("ti", [128, 2, H, TOP], U32)
        tf = sb("tf", [128, 2, H, TOP])
        cs = fo[:, :, 0:NCAND]
        ci_ = sb("ci", [128, H, NCAND])
        fv = tv[:, 0, :, :]
        fp = ti[:, 0, :, :]
        crest = rest[:, :, 0:NCAND]
        pwt = sb("pwt", [128, 2, H, TOP])
        psm = sb("psm", [128, 2, H])
        fx = tf[:, 0, :, :]
        ix = sb("ix", [128, 2, H, TOP], U32)
        gg = sb("gg", [128, GRING, HALF, 128])
        kv = sb("kv", [128, 2, H, D2])
        kvh = sb("kvh", [128, 2, D2])
        vf = sb("vf", [128, H, D2])
        ob = sb("ob", [128, 2, SIDE])
        wqs = sb("wqs", [128, 3, H * D1])
        wos = sb("wos", [128, 2, SIDE])
        bob = sb("bob", [128, SIDE])
        wpks = sb("wpks", [128, 512])
        keyb = sb("keyb", [128, 4, 256])
        wq2s = sb("wq2s", [128, 512])
        wo2s = sb("wo2s", [128, 4, SIDE])
        rel = sb("rel", [128, 128])
        relcls = sb("relcls", [128, H])
        mask = sb("mask", [128, 128])
        iota = sb("iota", [128, NCAND])
        headoff = sb("headoff", [128, H])
        k0b = sb("k0b", [128, 2, 4])
        v0 = sb("v0", [128, H, D1])
        kcb = sb("kcb", [128, 4, 2])
        vc = sb("vc", [128, H, D2])

        cvb = [pb_("cv0"), pb_("cv1")]
        tpb = pb_("tp")
        b3 = pb_("b3")
        b4 = pb_("b4")
        b5 = pb_("b5")
        wide = ctx.enter_context(nc.psum_tensor("wide", [128, 1024], F32))


        s_zero, s_const = sem("zeroed"), sem("constants_in")
        s_wi, s_neg, s_ws = sem("wi_in"), sem("wi_negated"), sem("wmix_out")
        s_grid = sem("grid_in")
        s_xl = [sem("pixels_in0"), sem("pixels_in1")]
        s_conv, s_lin, s_act = sem("conv_done"), sem("biased"), sem("rectified")
        s_fst, s_fold = sem("fold_y_done"), sem("fold_ready")
        s_off = [sem(f"offset_ready{i}") for i in range(GROUP)]
        s_tr, s_tt = sem("transposed"), sem("transposed_ready")
        s_fft, s_za, s_zd = sem("modes_done"), sem("modes_ready_even"), sem("modes_ready_odd")
        s_w = [sem(f"weights_in{i}") for i in range(WRING)]
        s_wchunk, s_mx = sem("weights_used"), sem("mixed_ready")
        s_mw = sem("mixed_out")
        s_mt, s_v, s_vt, s_vs = (sem("mode_rows_in"), sem("inv_y_done"), sem("inv_y_odd_ready"),
                                 sem("inv_y_ready"))
        s_q1, s_ql, s_qh, s_q2, s_rr, s_rows = (sem("hidden_done"), sem("hidden_biased"), sem("hidden_ready"), sem("head_done"),
                                          sem("rows_ready"), sem("rows_out"))
        s_ht = [sem(f"tokens_in{i}") for i in range(PAIRS)]
        s_ln, s_sd, s_xn, s_xtp, s_xt = (sem("ln_steps"), sem("std_ready"), sem("normed"), sem("normed_t_done"),
                                         sem("normed_t_ready"))
        s_qkp, s_qka, s_qkd = sem("qkv_done"), sem("qk_ready"), sem("v_ready")
        s_scp, s_sm1, s_ex1, s_ptp, s_pt = (sem("scores1_done"), sem("softmax1_steps"), sem("exp1_ready"),
                                            sem("probs1_t_done"), sem("probs1_t_ready"))
        s_pvp, s_ao, s_aop, s_aot, s_wop, s_h1 = (sem("pv1_done"), sem("attn1_steps"), sem("attn1_t_done"),
                                                  sem("attn1_t_ready"), sem("wo1_done"), sem("h1_steps"))
        s_qpp, s_qp, s_fq, s_smp, s_sim = (sem("qpk_done"), sem("qpk_ready"), sem("fq_ready"), sem("sim_done"),
                                           sem("sim_ready"))
        s_top, s_cst, s_pws, s_pwe, s_dst = (sem("top_steps"), sem("cand_steps"), sem("weight_steps"),
                                             sem("weight_exp"), sem("decode_steps"))
        s_g = [sem(f"gathered{i}") for i in range(2 * H)]
        s_mul, s_red, s_kv = sem("rows_weighted"), sem("rows_summed"), sem("kv_ready")
        s_vf, s_ktp, s_kt = sem("values_ready"), sem("keys_t_done"), sem("keys_t_ready")
        s_sc2, s_sm2, s_ex2, s_pt2p, s_pt2 = (sem("scores2_done"), sem("softmax2_steps"), sem("exp2_ready"),
                                              sem("probs2_t_done"), sem("probs2_t_ready"))
        s_pv2, s_fo, s_fop, s_fot, s_wo2, s_ob = (sem("pv2_done"), sem("attn2_steps"), sem("attn2_t_done"),
                                                  sem("attn2_t_ready"), sem("wo2_done"), sem("rows_final"))
        s_out = [sem("out_even"), sem("out_odd")]
        n_const = [0]

        s_met = {k: sem(f"wait_met_{k}") for k in ("pe", "dve", "pool")}

        def held(engine, name):
            engine.sem_inc(s_met[name], 1)

        U2 = 2 * UNITS
        A2 = 2 * LAYERS * GROUP
        FOLDS = LAYERS * GROUP
        QUADS = LAYERS * 2
        MB = NWCH // 2
        CHUNKS = LAYERS * NWCH
        PI = LAYERS * PAIRS
        LN, SM, TOPS, CS, PW, DEC = 6, 6, 8, 8, 4, 27

        def static(it):
            return isinstance(it, int)

        def tile_no(it, j):
            return 0 if static(it) and it == 0 else PAIRS * it + (j - PAIRS + 1)

        def steps(u, fno):
            s, i = divmod(u, GROUP)
            if not fno:
                return [u], []
            if s == 0:
                return [i // 2] if i % 2 else [], [GROUP // 2] if i == GROUP - 1 else []
            step = (GROUP + 1) * (s - 1) + GROUP // 2 + 1 + i
            return [step], [step + 1] if i == GROUP - 1 and s < LAYERS else []

        def tiles(it, now, tail):
            for j, step in [(j, step) for step in now for j in range(-3, PAIRS)]:
                r = step - SPAN * j
                if not 0 <= r <= R_OUT:
                    continue
                if static(it) and (it == 0 and j != 0 or it == 1 and j < 0) or tail and j >= 0:
                    continue
                yield j, r, static(it) and it == 0

        def older(it, j, k):
            return tile_no(it, j) - k >= 1 if static(it) else True

        def younger(it, j, k):
            return it > 0 and tile_no(it, j) + k <= IMGS // 2 if static(it) else True

        def iterations(engine, body):
            body(0, UNITS, True, False)
            body(1, UNITS, True, False)
            with engine.Fori(2, GROUPS) as it:
                body(it, UNITS, True, False)
            body(GROUPS, UNITS, False, False)
            body(GROUPS + 1, R_OUT - SPAN + 1, False, True)

        def image_ready(engine, it, u):
            if u < GROUP:
                engine.wait_ge(s_lin, U2 * it + 2 * u + 2)
            else:
                engine.wait_ge(s_act, A2 * it + 2 * (u - GROUP) + 2)

        def first(it):
            return static(it) and it == 0

        block = ctx.enter_context(nc.Block())

        @block.sync
        def _(sp):
            def const(dst, src):
                n_const[0] += 1
                sp.dma_start(dst, src).then_inc(s_const, 16)

            def col(v):
                return v.rearrange("(a b) -> a b", b=1)

            def row(v, n):
                return v.rearrange("(a b) -> a b", a=1).to_broadcast([128, n])

            sp.wait_ge(s_zero, 1)
            stage = tt[:, :, :, :, :].rearrange("k a b i c -> k (a b i c)")
            quarter = [(l, p, 64 * (l % 2) + 32 * p) for l in range(2) for p in range(2)]
            for c in range(4):
                if c:
                    sp.wait_ge(s_ws, 16 * 4 * c)
                cols = slice(HM * CH * (c % 2), HM * CH * (c % 2 + 1))
                for l, p, k in quarter:
                    sp.dma_start(stage[k:k + 32, :], wl[2 * (c // 2) + l, 64 * p + 32:64 * p + 64, cols]).then_inc(s_wi, 16)
                if c == 0:
                    const(ft[:, :, :], ft_c)
                    const(ident[:, :], ident_c)
                    for n, src in enumerate([pb] + [cb[l] for l in range(LAYERS)] + [q1b]):
                        for k in range(4):
                            const(bias[CH * k:CH * k + CH, n:n + 1], col(src))
                    for k in range(2):
                        const(bias[k:k + 1, 6:7], col(q2b))
                        const(bias[32 + k:33 + k, 6:7], col(q2b))
                    for k in range(4):
                        px, py = divmod(k, 2)
                        const(lw[3 * k:3 * k + 3, CH * k:CH * k + CH], pw[2:5, :])
                        const(lw[12 + 2 * k:14 + 2 * k, CH * k:CH * k + CH], pw[0:2, :])
                        const(q1[CH * k:CH * k + CH, CH * k:CH * k + CH], q1w)
                        const(q2[CH * k:CH * k + CH, 32 * px + py:32 * px + py + 1], q2w)
                    axis = [(u, o, a, 2 * u + o - a) for u in range(2) for o in range(2) for a in range(2)
                            if 0 <= 2 * u + o - a <= 2]
                    for u, qy, py, ty in axis:
                        for v, qx, px, tx in axis:
                            r0, c0 = 64 * qx + 32 * qy, 64 * px + 32 * py
                            const(cw[r0:r0 + 32, :, 2 * u + v, c0:c0 + 32], cwt[ty, tx])
                sp.wait_ge(s_neg, c + 1)
                for l, p, k in quarter:
                    sp.dma_start(wmix[2 * (c // 2) + l, 64 * p + 32:64 * p + 64, cols], stage[k:k + 32, :]).then_inc(s_ws, 16)
            for l in range(LAYERS):
                for p in range(2):
                    sp.dma_start(wmix[l, 64 * p:64 * p + 32, :], wl[l, 64 * p:64 * p + 32, :]).then_inc(s_ws, 16)
            const(i1[:, :, :], i1_c)
            const(i2[:, :, :], i2_c)
            for n, w in enumerate((wq, wk, wv)):
                const(wqs[0:SIDE, n, :], w)
            const(wos[:, :, :], wo.rearrange("(c k) n -> k c n", k=128))
            const(bob[:, :], row(bo, SIDE))
            const(wpks[0:SIDE, :], wqpk)
            const(wq2s[0:SIDE, :], wq2)
            const(wo2s[:, :, :], wo2.rearrange("(c k) n -> k c n", k=128))
            for p in range(2):
                for h in range(H):
                    k = h % 4
                    const(keyb[32 * k:32 * k + 32, 2 * p + h // 4, KEYS * k:KEYS * k + KEYS], keyst[p, h])
            const(rel[:, :], rel_c[0])
            const(mask[:, :], rel_c[1])
            const(relcls[:, :], relcls_c)
            const(iota[:, :], iota_c)
            const(headoff[:, :], head_c)
            const(ht[:, 0, :], cls.rearrange("a b c -> (a b) c").to_broadcast([128, SIDE]))
            sp.wait_ge(s_ws, 16 * (16 + 2 * LAYERS))

            def chunk(it, k):
                s, c = divmod(k, NWCH)
                if not (first(it) and k < WRING):
                    sp.wait_ge(s_wchunk, CHUNKS * it + (k - WRING + 1))
                sp.dma_start(wr[:, k % WRING, :], wmix[s, :, c * WCH * 2 * CH:(c + 1) * WCH * 2 * CH]).then_inc(s_w[k % WRING], 16)

            def mode_rows(it, s, b):
                sp.wait_ge(s_mx, LAYERS * MB * it + MB * (s - 1) + b + 1)
                for g in range(4):
                    src = mo[32 * g:32 * g + 2 * GROUP, 512 * b:512 * b + 512].rearrange("i (k c) -> i k c", c=2 * CH)
                    sp.dma_start(turned[32 * g + 8 * b:32 * g + 8 * b + 8].rearrange("k i c -> i k c"), src).then_inc(s_mw, 16)
                if b == MB - 1:
                    sp.wait_ge(s_mw, 64 * MB * (LAYERS * it + s))
                    sp.dma_start(mt[:, :, :, :, :].rearrange("k p i r c -> k (p i) (r c)"), turned).then_inc(s_mt, 16)

            def pixels(it, i):
                if i >= 2:
                    sp.wait_ge(s_conv, U2 * it + 2 * (i - 1))
                sp.dma_start(xl[0:12, i % 2, :], x12[GROUP * it + i]).then_inc(s_xl[i % 2], 16)

            def out_rows(it, i):
                sp.wait_ge(s_rr, 2 * GROUP * it + 2 * i + 2)
                r0 = (GROUP * it + i) * SIDE
                sp.dma_start(rows[bass.ds(r0, SIDE), :].rearrange("(y p) x -> p y x", p=2),
                             rr.rearrange("p (y x) -> p y x", x=SIDE)).then_inc(s_rows, 16)
                if i % 2:
                    j = i // 2
                    sp.wait_ge(s_rows, 16 * GROUP * it + 16 * (i + 1))
                    if not (first(it) and j > 0):
                        sp.wait_ge(s_h1, 2 * tile_no(it, j) + 2)
                    sp.dma_start(ht[:, j, :], rows[bass.ds((GROUP * it + i - 1) * SIDE, 2 * SIDE), :]).then_inc(s_ht[j], 16)

            def tile_out(it, j, is_cls):
                m = tile_no(it, j)
                sp.wait_ge(s_ob, m + 1)
                for e in range(2):
                    if is_cls:
                        half = slice(IMGS // 2 * e, IMGS // 2 * (e + 1))
                        sp.dma_start(out[half, 0, :], ob[half, 0, :]).then_inc(s_out[e], 16)
                    else:
                        sp.dma_start(out[2 * (m - 1) + e, 1:SIDE + 1, :],
                                     ob[64 * e:64 * e + 64, j % 2, :]).then_inc(s_out[j % 2], 16)

            def body(it, units, fno, tail):
                if fno:
                    if not first(it):
                        sp.wait_ge(s_conv, U2 * it)
                    for k in range(2):
                        sp.dma_start(xl[12:20, k, :], grid8).then_inc(s_grid, 16)
                    pixels(it, 0)
                    pixels(it, 1)
                for u in range(units):
                    s, i = divmod(u, GROUP)
                    if fno:
                        if i == 0 and s >= 1:
                            for c in range(WRING, NWCH):
                                chunk(it, NWCH * (s - 1) + c)
                                if c % 2:
                                    mode_rows(it, s, (c - WRING) // 2)
                            for b in range((NWCH - WRING) // 2, MB):
                                mode_rows(it, s, b)
                        if s < LAYERS:
                            image_ready(sp, it, u)
                            for px in range(2):
                                for py in range(2):
                                    src = 64 * px + 32 * py
                                    dst = 64 * (1 - px) + 32 * (1 - py)
                                    at = py * PITCH + px
                                    sp.dma_start(off[dst:dst + 32, i, at:at + HA_LEN],
                                                 ha[src:src + 32, u % 2, :]).then_inc(s_off[i], 16)
                            if i == GROUP - 1:
                                for c in range(WRING):
                                    chunk(it, NWCH * s + c)
                        if s == 0 and i + 2 < GROUP:
                            pixels(it, i + 2)
                        if s == LAYERS and i >= 1:
                            out_rows(it, i - 1)
                    for now in steps(u, fno):
                        for j, r, is_cls in tiles(it, now, tail):
                            if r == R_OUT:
                                tile_out(it, j, is_cls)
                if fno:
                    out_rows(it, GROUP - 1)

            iterations(sp, body)
            sp.wait_ge(s_out[0], 16 + 32 * (IMGS // 4))
            sp.wait_ge(s_out[1], 16 + 32 * (IMGS // 4))
            sp.wait_ge(s_rows, 16 * IMGS)
            sp.wait_ge(s_mw, 64 * MB * LAYERS * GROUPS)

        @block.gpsimd
        def _(pool):
            for t in (off[:, :, :], ha[:, :, :], cw[:, :, :, :], lw[:, :], q1[:, :], q2[:, :], kb[:, :, :, :], keyb[:, :, :], zz[:, :, :, :],
                      k0b[:, :, :], kcb[:, :, :], xnt[:, :], wqs[:, :, :], wpks[:, :], wq2s[:, :], bias[:, 0:7]):
                last = pool.memset(t, 0.0)
            pool.memset(bias[:, 7:8], EPS).then_inc(s_zero, 1)

            def gathers(it, j):
                m = tile_no(it, j)
                for q in range(2 * H):
                    h, half = divmod(q, 2)
                    if half == 0:
                        group = next(g for g in R_DEC.values() if g[0] <= h < g[1])
                        if h == group[0]:
                            pool.wait_ge(s_dst, DEC * m + 3 * group[1] + list(R_DEC.values()).index(group) + 1)
                    if not (first(it) and q < GRING):
                        pool.wait_ge(s_red, 2 * H * m + (q - GRING + 1 if q >= GRING else -((2 * H - 1 - q) % GRING)))
                    held(pool, "pool")
                    for k in range(HALF):
                        at = HALF * half + k
                        pool.indirect_dma_start(
                            out=gg[:, q % GRING, k, :], out_offset=None, in_=table,
                            in_offset=bass.IndirectOffsetOnAxis(ap=ix[:, j % 2, h, at:at + 1], axis=0),
                        ).then_inc(s_g[q], 16)

            gathers(0, 0)
            with pool.Fori(1, GROUPS + 1) as it:
                for j in range(PAIRS):
                    gathers(it, j)

        @block.tensor
        def _(pe):
            pe.wait_ge(s_const, 16 * n_const[0])
            mm = nc.tensor.matmul
            for bank in (b3, b4):
                mm(bank[:, :], ident[:, :], ft[:, 0:4, :].rearrange("k a m -> k (a m)"), start=True, stop=True)

            def transpose(dst, src):
                return mm(dst, src, ident[:, :], start=True, stop=True, is_transpose=True)

            def tap(it, u, hb, t):
                s, i = divmod(u, GROUP)
                a, b = divmod(t, 2)
                at = (16 * hb + a) * PITCH + b
                rhs = off[:, i, at:at + 16 * PITCH].rearrange("k (y x) -> k y x", x=PITCH)[:, :, 0:BLK]
                return mm(cvb[hb][:, :].rearrange("k (y x) -> k y x", x=BLK), cw[:, s - 1, t, :], rhs,
                          start=(t == 0), stop=(t == 3))

            def conv_begin(it, u, hb):
                s, i = divmod(u, GROUP)
                if not (first(it) and u == 0):
                    pe.wait_ge(s_lin, U2 * it + 2 * (u - 1) + hb + 1)
                if s == 0:
                    if hb == 0:
                        pe.wait_ge(s_grid, 32 * it + 32)
                        pe.wait_ge(s_xl[i % 2], 16 * 4 * it + 16 * (i // 2 + 1))
                    mm(cvb[hb][:, :], lw[0:20, :], xl[0:20, i % 2, 512 * hb:512 * hb + 512], start=True,
                       stop=True).then_inc(s_conv, 1)
                    return
                if hb == 0:
                    pe.wait_ge(s_off[i], 64 * LAYERS * it + 64 * s)
                for t in range(3):
                    tap(it, u, hb, t)

            def conv_end(it, u, hb):
                s, i = divmod(u, GROUP)
                if s == 0:
                    return
                if hb == 0:
                    pe.wait_ge(s_vs, 2 * PI * it + 8 * (s - 1) + 4 * (i // 4) + 4)
                for c in range(4):
                    for px in range(2):
                        mm(cvb[hb][64 * px:64 * px + 64, 128 * c:128 * c + 128],
                           vs[:, i // 4, i % 4, 4 * hb + c, :, :].rearrange("k a c -> k (a c)"),
                           i2[:, px, :], start=False, stop=False, skip_group_check=True)
                last = tap(it, u, hb, 3)
                last.then_inc(s_conv, 1)

            def turn(it, u, hb):
                if hb == 0:
                    pe.wait_ge(s_fold, FOLDS * it + u + 1)
                if u == 0 and hb == 0:
                    if not first(it):
                        pe.wait_ge(s_rr, 2 * GROUP * it)
                else:
                    pe.wait_ge(s_tt, 2 * FOLDS * it + 2 * u + hb)
                for c in range(4):
                    cc = 4 * hb + c
                    src = fold[:, cc // 4, (cc // 2) % 2, 8 * (cc % 2):8 * (cc % 2) + 8, :].rearrange("k y x -> k (y x)")
                    last = transpose(tpb[:, 128 * c:128 * c + 128], src)
                last.then_inc(s_tr, 1)

            def fft(it, s, q):
                pe.wait_ge(s_tt, 2 * FOLDS * it + 2 * (GROUP * s + 4 * q + 3) + 2)
                if q == 1:
                    pe.wait_ge(s_za, QUADS * it + 2 * s + 1)
                    pe.wait_ge(s_zd, QUADS * it + 2 * s + 1)
                elif s >= 1:
                    pe.wait_ge(s_vs, 2 * PI * it + 8 * s)
                for cl in range(4):
                    for a in range(2):
                        for b in range(4):
                            last = mm((b3, b4)[cl // 2][:, 128 * (cl % 2):128 * (cl % 2) + 128],
                                      tt[:, 2 * cl + a, b, :, :].rearrange("k i c -> k (i c)"),
                                      ft[:, 8 * cl + 4 * a + b, :], start=(a == 0 and b == 0), stop=(a == 1 and b == 3))
                last.then_inc(s_fft, 1)

            def mix(it, s):
                pe.wait_ge(s_za, QUADS * it + 2 * s)
                pe.wait_ge(s_zd, QUADS * it + 2 * s)
                if s >= 2:
                    pe.wait_ge(s_vs, 2 * PI * it + 8 * (s - 1))
                for c in range(NWCH):
                    k = NWCH * (s - 1) + c
                    if c % 2 == 0 and c >= 4:
                        pe.wait_ge(s_mx, LAYERS * MB * it + MB * (s - 1) + c // 2 - 1)
                    pe.wait_ge(s_w[k % WRING], 16 * (CHUNKS // WRING) * it + 16 * (k // WRING + 1))
                    held(pe, "pe")
                    for w in range(WCH):
                        g = w % 4
                        at = 2 * CH * (4 * (c % 2) + w // 4)
                        last = mm((b3, b4)[c // 2 % 2][32 * g:32 * g + 2 * GROUP, at:at + 2 * CH],
                                  zz[:, 32 * g + 4 * c + w // 4, :, :].rearrange("k p i -> k (p i)"),
                                  wr[:, k % WRING, 2 * CH * w:2 * CH * (w + 1)], start=True, stop=True)
                    last.then_inc(s_wchunk, 1)

            def inv_y(it, s, g):
                k, c = divmod(g, 4)
                if g >= 2:
                    pe.wait_ge(s_vs, 2 * PI * it + 8 * (s - 1) + g - 1)
                else:
                    pe.wait_ge(s_mt, 16 * (LAYERS * it + s))
                for p in range(2):
                    for py in range(2):
                        at = 128 * (2 * p + py)
                        for ri in range(2):
                            last = mm((b4, b3)[c % 2][:, at:at + 128], i1[:, 8 * (2 * p + ri) + 2 * c + py, :],
                                      mt[:, p, 4 * k:4 * k + 4, ri, :], start=(ri == 0), stop=(ri == 1))
                last.then_inc(s_v, 1)

            def hidden(it, i, hb):
                g = 2 * GROUP * it + 2 * i + hb
                image_ready(pe, it, LAYERS * GROUP + i)
                if i == 0 and hb == 0:
                    pe.wait_ge(s_tt, 2 * FOLDS * it + 2 * FOLDS)
                else:
                    pe.wait_ge(s_rr, g)
                rhs = ha[:, i % 2, 16 * hb * PITCH:16 * (hb + 1) * PITCH].rearrange("k (y x) -> k y x", x=PITCH)[:, :, 0:BLK]
                mm(tpb[:, :].rearrange("k (y x) -> k y x", x=BLK), q1[:, :], rhs, start=True, stop=True).then_inc(s_q1, 1)

            def scalars(it, i, hb):
                pe.wait_ge(s_qh, 2 * GROUP * it + 2 * i + hb + 1)
                mm(tpb[0:34, :], q2[:, :], qh[:, 512 * hb:512 * hb + 512], start=True, stop=True).then_inc(s_q2, 1)

            def unit(it, u, middle):
                s, i = divmod(u, GROUP)
                if s >= 1 and i == 0:
                    mix(it, s)
                    conv_begin(it, u, 0)
                    conv_begin(it, u, 1)
                    middle()
                    for g in range(4):
                        inv_y(it, s, g)
                    conv_end(it, u, 0)
                    conv_end(it, u, 1)
                    return
                head = s == LAYERS and i >= 1
                conv_begin(it, u, 0)
                if head:
                    hidden(it, i - 1, 0)
                middle()
                conv_end(it, u, 0)
                if s < LAYERS and i == 5:
                    fft(it, s, 0)
                if s >= 1 and i in (1, 2):
                    inv_y(it, s, 2 * i + 2)
                conv_begin(it, u, 1)
                if s < LAYERS and i >= 1:
                    turn(it, u - 1, 0)
                if head:
                    scalars(it, i - 1, 0)
                conv_end(it, u, 1)
                if head:
                    hidden(it, i - 1, 1)
                if s >= 1 and i in (1, 2):
                    inv_y(it, s, 2 * i + 3)
                if s < LAYERS and i >= 1:
                    turn(it, u - 1, 1)

            def unit_end(it, u):
                s, i = divmod(u, GROUP)
                if i == GROUP - 1 and s < LAYERS:
                    turn(it, u, 0)
                    turn(it, u, 1)
                    fft(it, s, 1)
                if i >= 1 and s == LAYERS:
                    scalars(it, i - 1, 1)
                if i == GROUP - 1 and s == LAYERS:
                    for hb in range(2):
                        hidden(it, i, hb)
                        scalars(it, i, hb)

            def tile_middle(it, j, r, is_cls):
                m = tile_no(it, j)
                n = m - 1
                old = lambda k: older(it, j, k)
                if r in (R_QKV, R_QPK):
                    k = int(r == R_QPK)
                    pe.wait_ge(s_xn, 2 * m + k + 1)
                    if k == 0 and old(3):
                        pe.wait_ge(s_fot, m - 2)
                    if static(it) and m == 1:
                        pe.wait_ge(s_ob, 1)
                    if k == 1:
                        pe.wait_ge(s_h1, 2 * m + 2)
                        if old(2):
                            pe.wait_ge(s_sm2, SM * (n - 2) + 1)
                    held(pe, "pe")
                    transpose(b5[0:SIDE, 0:128], xn[:, :]).then_inc(s_xtp, 1)

            def tile(it, j, r, is_cls):
                m = tile_no(it, j)
                n = m - 1
                old = lambda k: older(it, j, k)
                young = lambda k: younger(it, j, k)
                if r == R_QKV:
                    pe.wait_ge(s_xt, 2 * m + 1)
                    if not is_cls:
                        pe.wait_ge(s_sim, m)
                    for c in range(2):
                        for w in range(2):
                            mm(wide[:, 256 * w + 128 * c:256 * w + 128 * c + 128], wqs[:, w, 128 * c:128 * c + 128],
                               xnt[:, :], start=True, stop=True)
                    mm(wide[:, 512:768], xnt[:, :], wqs[:, 2, :], start=True, stop=True).then_inc(s_qkp, 1)
                elif r == R_SC1 and not is_cls:
                    pe.wait_ge(s_qka, m + 1)
                    pe.wait_ge(s_qkd, m + 1)
                    if old(3):
                        pe.wait_ge(s_ob, m - 2)
                    for c in range(2):
                        mm(wide[:, 512 * c:512 * c + 512], qt[:, c, :], kb[:, c, :, :].rearrange("k h s -> k (h s)"),
                           start=True, stop=True)
                    for c in range(2):
                        last = mm(b5[:, 4 * c:4 * c + 4], qt[:, c, :], k0b[:, c, :], start=True, stop=True)
                    last.then_inc(s_scp, 1)
                elif r in (R_PT1, R_PT2) and not is_cls:
                    pe.wait_ge(s_ex1 if r == R_PT1 else s_ex2, n + 1)
                    for h in range(H):
                        last = transpose(wide[:, 128 * h:128 * h + 128], ee[:, h, 0:128])
                    last.then_inc(s_ptp if r == R_PT1 else s_pt2p, 1)
                elif r == R_PV1 and not is_cls:
                    pe.wait_ge(s_pt, n + 1)
                    for h in range(H):
                        last = mm(b5[:, D1 * h:D1 * h + D1], pt[:, h, :], vv[:, h, :], start=True, stop=True)
                    last.then_inc(s_pvp, 1)
                elif r == R_AOT:
                    if is_cls:
                        pe.wait_ge(s_qkd, 1)
                    else:
                        pe.wait_ge(s_ao, 3 * n + 3)
                    src = v0 if is_cls else ao
                    for c in range(2):
                        last = transpose(b5[:, 128 * c:128 * c + 128], src[:, 4 * c:4 * c + 4, :].rearrange("t h d -> t (h d)"))
                    last.then_inc(s_aop, 1)
                elif r == R_WO1:
                    pe.wait_ge(s_aot, m + 1)
                    if old(2):
                        pe.wait_ge(s_kt, m - 1)
                    for c in range(2):
                        last = mm(b5[:, 0:SIDE], aot[:, c, :], wos[:, c, :], start=(c == 0), stop=(c == 1))
                    last.then_inc(s_wop, 1)
                elif r == R_QPK:
                    pe.wait_ge(s_xt, 2 * m + 2)
                    if old(2):
                        pe.wait_ge(s_pt2, n - 1)
                    for c in range(4):
                        mm(wide[:, 128 * c:128 * c + 128], wpks[:, 128 * c:128 * c + 128], xnt[:, :], start=True, stop=True)
                    for c in range(4):
                        last = mm(wide[:, 512 + 128 * c:640 + 128 * c], wq2s[:, 128 * c:128 * c + 128], xnt[:, :],
                                  start=True, stop=True)
                    last.then_inc(s_qpp, 1)
                elif r == R_SIM:
                    pe.wait_ge(s_qp, m + 1)
                    pe.wait_ge(s_fq, m + 1)
                    for c in range(4):
                        last = mm(wide[:, 256 * c:256 * c + 256], qk[:, c, :], keyb[:, c, :], start=True, stop=True)
                    last.then_inc(s_smp, 1)
                elif r == R_KT:
                    pe.wait_ge(s_kv, H * m + H)
                    if young(2):
                        pe.wait_ge(s_aot, m + 3)
                    for c in range(4):
                        last = transpose(b5[:, 128 * c:128 * c + 128], kv[:, 0, 2 * c:2 * c + 2, :].rearrange("t h d -> t (h d)"))
                    last.then_inc(s_ktp, 1)
                elif r == R_SC2 and not is_cls:
                    pe.wait_ge(s_kt, m + 1)
                    if young(2):
                        pe.wait_ge(s_pt, n + 3)
                        pe.wait_ge(s_h1, 2 * m + 6)
                    for e in range(2):
                        for c in range(4):
                            mm(wide[:, 512 * e + 128 * c:512 * e + 128 * c + 128], fq[64 * e:64 * e + 64, j % 2, c, :],
                               qk[64 * e:64 * e + 64, c, :], start=True, stop=True)
                    for c in range(4):
                        last = mm(b5[:, 2 * c:2 * c + 2], fq[:, j % 2, c, :], kcb[:, c, :], start=True, stop=True)
                    last.then_inc(s_sc2, 1)
                elif r == R_PV2 and not is_cls:
                    pe.wait_ge(s_pt2, n + 1)
                    pe.wait_ge(s_vf, m + 1)
                    if young(2):
                        pe.wait_ge(s_xt, 2 * m + 6)
                    for h in range(H):
                        last = mm(b5[:, D2 * h:D2 * h + D2], pt[:, h, :], vf[:, h, :], start=True, stop=True)
                    last.then_inc(s_pv2, 1)
                elif r == R_FOT:
                    if is_cls:
                        pe.wait_ge(s_vf, 1)
                    else:
                        pe.wait_ge(s_fo, 2 * n + 2)
                    src = vc if is_cls else fo
                    for c in range(4):
                        last = transpose(b5[:, 128 * c:128 * c + 128], src[:, 2 * c:2 * c + 2, :].rearrange("t h d -> t (h d)"))
                    last.then_inc(s_fop, 1)
                elif r == R_WO2:
                    pe.wait_ge(s_fot, m + 1)
                    if young(3):
                        pe.wait_ge(s_xt, 2 * m + 7)
                    for c in range(4):
                        last = mm(b5[:, 0:SIDE], aot[:, c, :], wo2s[:, c, :], start=(c == 0), stop=(c == 3))
                    last.then_inc(s_wo2, 1)

            def body(it, units, fno, tail):
                def middle(now):
                    for j, r, is_cls in tiles(it, now, tail):
                        tile_middle(it, j, r, is_cls)

                for u in range(units):
                    now, later = steps(u, fno)
                    if fno:
                        unit(it, u, lambda: middle(now))
                    else:
                        middle(now)
                    for j, r, is_cls in tiles(it, now, tail):
                        tile(it, j, r, is_cls)
                    if fno:
                        unit_end(it, u)
                    middle(later)
                    for j, r, is_cls in tiles(it, later, tail):
                        tile(it, j, r, is_cls)

            iterations(pe, body)

        @block.scalar
        def _(act):
            fn = nc.scalar.activation
            stage = tt[:, :, :, :, :].rearrange("k a b i c -> k (a b i c)")
            for c in range(4):
                act.wait_ge(s_wi, 16 * 4 * (c + 1))
                part = stage.rearrange("k (m r c) -> k m r c", r=2, c=CH)[:, :, 0, :]
                fn(part, part, ACT.Copy, scale=-1.0).then_inc(s_neg, 1)
            act.wait_ge(s_const, 16 * n_const[0])
            act.wait_ge(s_ws, 16 * (16 + 2 * LAYERS))

            def aligned(it, u, hb):
                s, i = divmod(u, GROUP)
                act.wait_ge(s_conv, U2 * it + 2 * u + hb + 1)
                if hb == 0:
                    v = u - 2
                    if v >= 0 and v < FOLDS:
                        act.wait_ge(s_fst, 3 * FOLDS * it + 3 * v + 3)
                        act.wait_ge(s_off[v % GROUP], 64 * LAYERS * it + 64 * (v // GROUP + 1))
                    elif v >= FOLDS or not first(it):
                        act.wait_ge(s_q1, 2 * GROUP * it + 2 * (v - FOLDS + 1) if v >= 0 else 2 * GROUP * it + 2 * (v + 1))
                dst = ha[:, u % 2, 16 * hb * PITCH:16 * (hb + 1) * PITCH].rearrange("k (y x) -> k y x", x=PITCH)[:, :, 0:BLK]
                fn(dst, cvb[hb][:, :].rearrange("k (y x) -> k y x", x=BLK), ACT.Identity,
                   bias=bias[:, s:s + 1]).then_inc(s_lin, 1)

            def turned(it, u, hb):
                s, i = divmod(u, GROUP)
                act.wait_ge(s_tr, 2 * FOLDS * it + 2 * u + hb + 1)
                if hb == 0 and i % 4 == 0:
                    if u == 0:
                        if not first(it):
                            act.wait_ge(s_rows, 16 * GROUP * it)
                    else:
                        act.wait_ge(s_fft, QUADS * it + 2 * s + i // 4)
                dst = tt[:, 4 * hb:4 * hb + 4, :, i % 4, :].rearrange("k a b c -> k (a b) c")
                fn(dst, tpb[:, :].rearrange("k (a c) -> k a c", c=CH), ACT.Copy).then_inc(s_tt, 1)

            def modes(it, s, q):
                act.wait_ge(s_fft, QUADS * it + 2 * s + q + 1)
                for i in range(4):
                    for ri in range(2):
                        src = b3[32 * i:32 * i + 32, 0:256].rearrange("k (q r m) -> k q r m", q=2, r=2)[:, :, ri, :]
                        dst = zz[32 * ri:32 * ri + 32, :, 0, 4 * q + i].rearrange("k (q m) -> k q m", q=2)
                        last = fn(dst, src, ACT.Copy)
                last.then_inc(s_za, 1)

            def mixed(it, s, b):
                act.wait_ge(s_wchunk, CHUNKS * it + NWCH * (s - 1) + 2 * (b + 1))
                fn(mo[:, 512 * b:512 * b + 512], (b3, b4)[b % 2][:, :], ACT.Copy).then_inc(s_mx, 1)

            def inv_y(it, s, k):
                g = 8 * (s - 1) + k
                act.wait_ge(s_v, 2 * PI * it + g + 1)
                if g or not first(it):
                    act.wait_ge(s_vs, 2 * PI * it + g)
                fn(vt[:, :, :, :].rearrange("k b i c -> k (b i c)"), (b4, b3)[k % 2][:, 256:512], ACT.Copy).then_inc(s_vt, 1)

            def hidden(it, i, hb):
                g = 2 * GROUP * it + 2 * i + hb
                act.wait_ge(s_q1, g + 1)
                if i == 0 and hb == 0:
                    act.wait_ge(s_tr, 2 * FOLDS * it + 2 * FOLDS)
                if i:
                    act.wait_ge(s_q2, g - 1)
                fn(qh[:, 512 * hb:512 * hb + 512], tpb[:, :], ACT.Identity, bias=bias[:, 5:6]).then_inc(s_ql, 1)

            def token_rows(it, i, hb):
                act.wait_ge(s_q2, 2 * GROUP * it + 2 * i + hb + 1)
                if i and hb == 0:
                    act.wait_ge(s_rows, 16 * GROUP * it + 16 * i)
                for px in range(2):
                    dst = rr[:, 1024 * hb:1024 * hb + 1024].rearrange("p (n x) -> p n x", x=2)[:, :, px]
                    last = fn(dst, tpb[32 * px:32 * px + 2, :], ACT.Identity, bias=bias[32 * px:32 * px + 2, 6:7])
                last.then_inc(s_rr, 1)

            def unit(it, u, middle):
                s, i = divmod(u, GROUP)
                if s >= 1 and i == 0:
                    for b in range(MB):
                        mixed(it, s, b)
                    for g in range(4):
                        inv_y(it, s, g)
                head = s == LAYERS and i >= 1
                if head:
                    hidden(it, i - 1, 0)
                aligned(it, u, 0)
                if s < LAYERS and i == 5:
                    modes(it, s, 0)
                if s >= 1 and i in (1, 2):
                    inv_y(it, s, 2 * i + 2)
                if head:
                    token_rows(it, i - 1, 0)
                if s < LAYERS and i >= 1:
                    turned(it, u - 1, 0)
                middle()
                aligned(it, u, 1)
                if head:
                    hidden(it, i - 1, 1)
                if s >= 1 and i in (1, 2):
                    inv_y(it, s, 2 * i + 3)
                if s < LAYERS and i >= 1:
                    turned(it, u - 1, 1)

            def unit_end(it, u):
                s, i = divmod(u, GROUP)
                if i == GROUP - 1 and s < LAYERS:
                    turned(it, u, 0)
                    turned(it, u, 1)
                    modes(it, s, 1)
                if i >= 1 and s == LAYERS:
                    token_rows(it, i - 1, 1)
                if i == GROUP - 1 and s == LAYERS:
                    for hb in range(2):
                        hidden(it, i, hb)
                        token_rows(it, i, hb)

            def copies(dst, src, done, scale=1.0):
                fn(dst, src, ACT.Copy, scale=scale).then_inc(done, 1)

            def tile_middle(it, j, r, is_cls):
                m = tile_no(it, j)
                n = m - 1
                if r in (R_XT1, R_XT2):
                    k = int(r == R_XT2)
                    act.wait_ge(s_ln, LN * m + 3 * k + 2)
                    fn(lnst[:, k, 8:9], lnst[:, k, 7:8], ACT.Sqrt, bias=bias[:, 7:8]).then_inc(s_sd, 1)
                elif r in (R_QKV, R_QPK):
                    k = int(r == R_QPK)
                    act.wait_ge(s_xtp, 2 * m + k + 1)
                    if k:
                        act.wait_ge(s_qkp, m + 1)
                    elif not is_cls:
                        act.wait_ge(s_qpp, m)
                    copies(xnt[0:SIDE, :], b5[0:SIDE, 0:128], s_xt)
                elif r in (R_PT1, R_PT2) and not is_cls:
                    one = r == R_PT1
                    act.wait_ge(s_sm1 if one else s_sm2, SM * n + 3)
                    fn(ee[:, :, :].rearrange("t h s -> t (h s)"), ee[:, :, :].rearrange("t h s -> t (h s)"), ACT.Exp)\
                        .then_inc(s_ex1 if one else s_ex2, 1)
                elif r == R_SOFT:
                    act.wait_ge(s_pws, PW * m + 1)
                    w = pwt[:, j % 2, :, :].rearrange("t h k -> t (h k)")
                    fn(w, w, ACT.Exp).then_inc(s_pwe, 1)

            def tile(it, j, r, is_cls):
                m = tile_no(it, j)
                n = m - 1
                old = lambda k: older(it, j, k)
                young = lambda k: younger(it, j, k)
                if r == R_QKV:
                    act.wait_ge(s_qkp, m + 1)
                    src = wide[:, 256:512].rearrange("k (c t) -> k c t", c=2)
                    if is_cls:
                        for a in range(4):
                            last = fn(k0b[32 * a:32 * a + 32, :, a], src[32 * a:32 * a + 32, :, 0], ACT.Copy)
                    else:
                        if old(1):
                            act.wait_ge(s_scp, n)
                        fn(qt[:, :, :].rearrange("k c t -> k (c t)"), wide[:, 0:256], ACT.Copy, scale=float(D1) ** -0.5)
                        for a in range(4):
                            last = fn(kb[32 * a:32 * a + 32, :, a, :], src[32 * a:32 * a + 32, :, :], ACT.Copy)
                    last.then_inc(s_qka, 1)
                elif r in (R_PT1, R_PT2) and not is_cls:
                    one = r == R_PT1
                    act.wait_ge(s_ptp if one else s_pt2p, n + 1)
                    if one and old(3):
                        act.wait_ge(s_pv2, n - 2)
                    if not one and young(2):
                        act.wait_ge(s_pvp, n + 3)
                    for c in range(2):
                        last = fn(pt[:, 4 * c:4 * c + 4, :].rearrange("s h t -> s (h t)"), wide[:, 512 * c:512 * c + 512], ACT.Copy)
                    last.then_inc(s_pt if one else s_pt2, 1)
                elif r == R_AOT:
                    act.wait_ge(s_aop, m + 1)
                    if old(3):
                        act.wait_ge(s_wo2, m - 2)
                    copies(aot[:, 0:2, :].rearrange("k c t -> k (c t)"), b5[:, 0:256], s_aot)
                elif r == R_QPK:
                    act.wait_ge(s_qpp, m + 1)
                    if old(2):
                        act.wait_ge(s_sc2, n - 1)
                    copies(qk[:, :, :].rearrange("k c t -> k (c t)"), wide[:, 0:512], s_qp)
                    copies(fq[:, j % 2, :, :].rearrange("k c t -> k (c t)"), wide[:, 512:1024], s_fq, float(D2) ** -0.5)
                elif r == R_SIM:
                    act.wait_ge(s_smp, m + 1)
                    if not is_cls:
                        act.wait_ge(s_dst, DEC * m)
                    if old(2):
                        act.wait_ge(s_pt2p, n - 1)
                        act.wait_ge(s_sm2, SM * (n - 2) + 6)
                    for c in range(2):
                        last = fn(sim[:, 8 * c:8 * c + 8, :].rearrange("t g k -> t (g k)"), wide[:, 512 * c:512 * c + 512], ACT.Copy)
                    last.then_inc(s_sim, 1)
                elif r == R_KT:
                    act.wait_ge(s_ktp, m + 1)
                    if is_cls:
                        for e in range(2):
                            last = fn(kcb[64 * e:64 * e + 64, :, e], b5[64 * e:64 * e + 64, :]
                                      .rearrange("k (c t) -> k c t", c=4)[:, :, 0], ACT.Copy)
                        last.then_inc(s_kt, 1)
                    else:
                        if young(1):
                            act.wait_ge(s_smp, m + 2)
                        copies(qk[:, :, :].rearrange("k c t -> k (c t)"), b5[:, :], s_kt)
                elif r == R_FOT:
                    act.wait_ge(s_fop, m + 1)
                    if young(2):
                        act.wait_ge(s_wop, m + 3)
                    copies(aot[:, :, :].rearrange("k c t -> k (c t)"), b5[:, :], s_fot)

            def body(it, units, fno, tail):
                def middle(now):
                    for j, r, is_cls in tiles(it, now, tail):
                        tile_middle(it, j, r, is_cls)

                for u in range(units):
                    now, later = steps(u, fno)
                    if fno:
                        unit(it, u, lambda: middle(now))
                    else:
                        middle(now)
                    for j, r, is_cls in tiles(it, now, tail):
                        tile(it, j, r, is_cls)
                    if fno:
                        unit_end(it, u)
                    middle(later)
                    for j, r, is_cls in tiles(it, later, tail):
                        tile(it, j, r, is_cls)

            iterations(act, body)

        @block.vector
        def _(dve):
            v = nc.vector
            dve.wait_ge(s_const, 16 * n_const[0])

            def inv_y(it, s, g):
                dve.wait_ge(s_vt, 2 * PI * it + 8 * (s - 1) + g + 1)
                k, c = divmod(g, 4)
                even = (b4, b3)[c % 2][:, 0:256].rearrange("k (b i c) -> k b i c", b=2, i=4)
                for low, op in ((0, ALU.add), (4, ALU.subtract)):
                    last = v.tensor_tensor(vs[:, k, :, low + c, :, :].rearrange("k i b c -> k b i c"), even, vt[:, :, :, :], op)
                last.then_inc(s_vs, 1)

            def folds(it, u):
                image_ready(dve, it, u)
                if u == 0 and not first(it):
                    dve.wait_ge(s_q2, 2 * GROUP * it)
                img = ha[:, u % 2, :].rearrange("k (y x) -> k y x", x=PITCH)
                base = 3 * FOLDS * it + 3 * u
                if u or not first(it):
                    dve.wait_ge(s_fold, FOLDS * it + u)
                for p, op in ((0, ALU.add), (1, ALU.subtract)):
                    if p:
                        dve.wait_ge(s_fst, base + 2)
                    v.tensor_tensor(fold1[:, :, :], img[:, 0:16, 0:BLK], img[:, 16:32, 0:BLK], op).then_inc(s_fst, 1)
                    dve.wait_ge(s_fst, base + 2 * p + 1)
                    if u or not first(it):
                        dve.wait_ge(s_tr, 2 * FOLDS * it + 2 * u - 1 + p)
                    for q, op2 in ((0, ALU.add), (1, ALU.subtract)):
                        last = v.tensor_tensor(fold[:, p, q, :, :], fold1[:, :, 0:16], fold1[:, :, 16:32], op2)
                    if p == 0:
                        last.then_inc(s_fst, 1)
                last.then_inc(s_fold, 1)

            def modes(it, s, q):
                dve.wait_ge(s_fft, QUADS * it + 2 * s + q + 1)
                for i in range(4):
                    for ri in range(2):
                        src = b4[32 * i:32 * i + 32, 0:256].rearrange("k (q r m) -> k q r m", q=2, r=2)[:, :, ri, :]
                        dst = zz[64 + 32 * ri:96 + 32 * ri, :, 1, 4 * q + i].rearrange("k (q m) -> k q m", q=2)
                        last = v.tensor_copy(dst, src)
                last.then_inc(s_zd, 1)

            def rectified(it, u, hb):
                dve.wait_ge(s_lin, U2 * it + 2 * u + hb + 1)
                img = ha[:, u % 2, 16 * hb * PITCH:16 * (hb + 1) * PITCH].rearrange("k (y x) -> k y x", x=PITCH)[:, :, 0:BLK]
                v.scalar_tensor_tensor(img, img, SLOPE, img, ALU.mult, ALU.max).then_inc(s_act, 1)

            def hidden(it, i, hb):
                dve.wait_ge(s_ql, 2 * GROUP * it + 2 * i + hb + 1)
                part = qh[:, 512 * hb:512 * hb + 512]
                v.scalar_tensor_tensor(part, part, SLOPE, part, ALU.mult, ALU.max).then_inc(s_qh, 1)

            def unit(it, u, middle):
                s, i = divmod(u, GROUP)
                if s >= 1 and i == 0:
                    for g in range(4):
                        inv_y(it, s, g)
                if s == LAYERS and i >= 1:
                    hidden(it, i - 1, 0)
                if s >= 1:
                    rectified(it, u, 0)
                if s < LAYERS and i == 5:
                    modes(it, s, 0)
                if s >= 1 and i in (1, 2):
                    inv_y(it, s, 2 * i + 2)
                middle()
                if s >= 1:
                    rectified(it, u, 1)
                if s == LAYERS and i >= 1:
                    hidden(it, i - 1, 1)
                if s >= 1 and i in (1, 2):
                    inv_y(it, s, 2 * i + 3)
                if s < LAYERS:
                    folds(it, u)

            def unit_end(it, u):
                s, i = divmod(u, GROUP)
                if i == GROUP - 1 and s < LAYERS:
                    modes(it, s, 1)
                if i == GROUP - 1 and s == LAYERS:
                    for hb in range(2):
                        hidden(it, i, hb)

            def layer_stats(m, k, src, is_cls):
                base = LN * m + 3 * k
                if not is_cls:
                    dve.wait_ge(s_ln, LN * m)
                    dve.wait_ge(s_xn, 2 * m)
                v.bn_stats(lnst[:, k, 0:6], src).then_inc(s_ln, 1)
                dve.wait_ge(s_ln, base + 1)
                held(dve, "dve")
                v.bn_aggr(lnst[:, k, 6:8], lnst[:, k, 0:6]).then_inc(s_ln, 1)

            def normed(m, k, src, is_cls):
                dve.wait_ge(s_sd, 2 * m + k + 1)
                v.reciprocal(lnst[:, k, 9:10], lnst[:, k, 8:9]).then_inc(s_ln, 1)
                dve.wait_ge(s_ln, LN * m + 3 * k + 3)
                if k or not is_cls:
                    dve.wait_ge(s_xtp, 2 * m + k)
                v.tensor_scalar(xn[:, :], src, lnst[:, k, 6:7], lnst[:, k, 9:10], ALU.subtract, ALU.mult).then_inc(s_xn, 1)

            def shares(a, n, ex, steps):
                dve.wait_ge(ex, n + 1)
                v.tensor_reduce(smx[:, a, 1, :], ee[:, :, :], AX.X, ALU.add).then_inc(steps, 1)
                dve.wait_ge(steps, SM * n + 4)
                v.reciprocal(smx[:, a, 2, :], smx[:, a, 1, :]).then_inc(steps, 1)
                dve.wait_ge(steps, SM * n + 5)
                v.tensor_tensor(smx[:, a, 3, :], ee[:, :, 128], smx[:, a, 2, :], ALU.mult).then_inc(steps, 1)

            def shift(it, a, n, steps):
                if not (static(it) and n == 0):
                    dve.wait_ge(s_fo if a else s_ao, 2 * n if a else 3 * n)
                dve.wait_ge(steps, SM * n + 1)
                v.tensor_reduce(smx[:, a, 0, :], ee[:, :, :], AX.X, ALU.max).then_inc(steps, 1)
                dve.wait_ge(steps, SM * n + 2)
                v.tensor_tensor(ee[:, :, :], ee[:, :, :], smx[:, a, 0, :].unsqueeze(2).to_broadcast([128, H, 129]),
                                ALU.subtract).then_inc(steps, 1)

            def tile_middle(it, j, r, is_cls):
                m = tile_no(it, j)
                if r in (R_XT1, R_XT2):
                    k = int(r == R_XT2)
                    normed(m, k, (h1 if k else ht)[:, j % PAIRS, :], is_cls)

            def tile(it, j, r, is_cls):
                m = tile_no(it, j)
                n = m - 1
                old = lambda k: older(it, j, k)
                young = lambda k: younger(it, j, k)
                if r == R_LN1:
                    if not is_cls:
                        dve.wait_ge(s_ht[j % PAIRS], 16 * it)
                    layer_stats(m, 0, ht[:, j % PAIRS, :], is_cls)
                elif r == R_QKV:
                    dve.wait_ge(s_qkp, m + 1)
                    v.tensor_copy((v0 if is_cls else vv)[:, :, :].rearrange("t h d -> t (h d)"), wide[:, 512:768]).then_inc(s_qkd, 1)
                elif r == R_SC1 and not is_cls:
                    dve.wait_ge(s_scp, n + 1)
                    dve.wait_ge(s_top, TOPS * m)
                    for h in range(H):
                        v.scalar_tensor_tensor(ee[:, h, 0:128], rel[:, :], 0.5 ** (h + 1), wide[:, 128 * h:128 * h + 128],
                                               ALU.mult, ALU.add)
                    v.tensor_tensor(ee[:, :, 128], b5[:, 0:H], relcls[:, :], ALU.add).then_inc(s_sm1, 1)
                    shift(it, 0, n, s_sm1)
                elif r == R_PT1 and not is_cls:
                    shares(0, n, s_ex1, s_sm1)
                elif r == R_PV1 and not is_cls:
                    dve.wait_ge(s_pvp, n + 1)
                    dve.wait_ge(s_sm1, SM * n + 6)
                    wide1 = [128, H, D1]
                    dve.wait_ge(s_cst, CS * m)
                    if old(3):
                        dve.wait_ge(s_fo, 2 * n - 4)
                    v.tensor_tensor(atmp, v0[:, :, :], smx[:, 0, 3, :].unsqueeze(2).to_broadcast(wide1), ALU.mult).then_inc(s_ao, 1)
                    if old(3):
                        dve.wait_ge(s_fop, m - 2)
                    v.tensor_tensor(ao, b5[:, 0:256].rearrange("t (h d) -> t h d", h=H),
                                    smx[:, 0, 2, :].unsqueeze(2).to_broadcast(wide1), ALU.mult).then_inc(s_ao, 1)
                    dve.wait_ge(s_ao, 3 * n + 2)
                    v.tensor_tensor(ao, ao, atmp, ALU.add).then_inc(s_ao, 1)
                elif r == R_WO1:
                    slot = j % PAIRS
                    if not static(it) or m == 1 or m >= 5:
                        dve.wait_ge(s_ob, 1 if static(it) and m == 1 else m - 3)
                    v.tensor_tensor(h1[:, slot, :], ht[:, slot, :], bob[:, :], ALU.add).then_inc(s_h1, 1)
                    dve.wait_ge(s_wop, m + 1)
                    dve.wait_ge(s_h1, 2 * m + 1)
                    v.tensor_tensor(h1[:, slot, :], h1[:, slot, :], b5[:, 0:SIDE], ALU.add).then_inc(s_h1, 1)
                    dve.wait_ge(s_h1, 2 * m + 2)
                    layer_stats(m, 1, h1[:, slot, :], is_cls)
                elif r in (R_TOP0, R_TOP1):
                    p = int(r == R_TOP1)
                    base = TOPS * m + 4 * p
                    if p or not is_cls:
                        dve.wait_ge(s_top, base)
                    if p == 0 and not is_cls:
                        dve.wait_ge(s_dst, DEC * m)
                        dve.wait_ge(s_cst, CS * m)
                        dve.wait_ge(s_ao, 3 * n + 3)
                        if old(2):
                            dve.wait_ge(s_fo, 2 * n - 2)
                    dve.wait_ge(s_sim, m + 1)
                    held(dve, "dve")
                    for h in range(H):
                        last = v.max(tv[:, p, h, 0:8], sim[:, H * p + h, :])
                    last.then_inc(s_top, 1)
                    dve.wait_ge(s_top, base + 1)
                    held(dve, "dve")
                    for h in range(H):
                        v.max_index(ti[:, p, h, 0:8], tv[:, p, h, 0:8], sim[:, H * p + h, :])
                        last = v.match_replace(rest[:, h, :], tv[:, p, h, 0:8], sim[:, H * p + h, :], LOW)
                    last.then_inc(s_top, 1)
                    dve.wait_ge(s_top, base + 2)
                    held(dve, "dve")
                    for h in range(H):
                        last = v.max(tv[:, p, h, 8:16], rest[:, h, :])
                    last.then_inc(s_top, 1)
                    dve.wait_ge(s_top, base + 3)
                    held(dve, "dve")
                    for h in range(H):
                        last = v.max_index(ti[:, p, h, 8:16], tv[:, p, h, 8:16], rest[:, h, :])
                    last.then_inc(s_top, 1)
                elif r == R_CAND:
                    base = CS * m
                    dve.wait_ge(s_top, TOPS * m + 8)
                    if not is_cls:
                        dve.wait_ge(s_dst, DEC * m)
                        dve.wait_ge(s_pws, PW * m)
                        dve.wait_ge(s_aop, m + 1)
                        if not (static(it) and m < 2):
                            dve.wait_ge(s_mul, 2 * H * (m - 1))
                    v.tensor_tensor(tf[:, 0, :, :], ti[:, 0, :, :], headoff[:, :].unsqueeze(2).to_broadcast([128, H, TOP]), ALU.add)
                    v.tensor_scalar(tf[:, 1, :, :], ti[:, 1, :, :], float(KEYS), None, ALU.mult).then_inc(s_cst, 1)
                    dve.wait_ge(s_cst, base + 1)
                    if old(2):
                        dve.wait_ge(s_fop, m - 1)
                    at = 0
                    for a, na, nb in CAND:
                        for dst, src in ((cs, tv), (ci_, tf)):
                            last = v.tensor_tensor(
                                dst[:, :, at:at + na * nb].rearrange("t h (a b) -> t h a b", b=nb),
                                src[:, 0, :, a:a + na].unsqueeze(3).to_broadcast([128, H, na, nb]),
                                src[:, 1, :, 0:nb].unsqueeze(2).to_broadcast([128, H, na, nb]), ALU.add)
                        at += na * nb
                    last.then_inc(s_cst, 1)
                    dve.wait_ge(s_cst, base + 2)
                    held(dve, "dve")
                    for h in range(H):
                        last = v.max(fv[:, h, 0:8], cs[:, h, :])
                    last.then_inc(s_cst, 1)
                    dve.wait_ge(s_cst, base + 3)
                    held(dve, "dve")
                    for h in range(H):
                        v.max_index(fp[:, h, 0:8], fv[:, h, 0:8], cs[:, h, :])
                        last = v.match_replace(crest[:, h, :], fv[:, h, 0:8], cs[:, h, :], LOW)
                    last.then_inc(s_cst, 1)
                    dve.wait_ge(s_cst, base + 4)
                    held(dve, "dve")
                    for h in range(H):
                        last = v.max(fv[:, h, 8:16], crest[:, h, :])
                    last.then_inc(s_cst, 1)
                    dve.wait_ge(s_cst, base + 5)
                    v.tensor_tensor(pwt[:, j % 2, :, :], fv[:, :, :], fv[:, :, 0:1].to_broadcast([128, H, TOP]),
                                    ALU.subtract).then_inc(s_pws, 1)
                    for h in range(H):
                        last = v.max_index(fp[:, h, 8:16], fv[:, h, 8:16], crest[:, h, :])
                    last.then_inc(s_cst, 3)
                elif r == R_SOFT:
                    dve.wait_ge(s_pwe, m + 1)
                    w = pwt[:, j % 2, :, :]
                    v.tensor_reduce(psm[:, 0, :], w, AX.X, ALU.add).then_inc(s_pws, 1)
                    dve.wait_ge(s_pws, PW * m + 2)
                    v.reciprocal(psm[:, 1, :], psm[:, 0, :]).then_inc(s_pws, 1)
                    dve.wait_ge(s_pws, PW * m + 3)
                    v.tensor_tensor(w, w, psm[:, 1, :].unsqueeze(2).to_broadcast([128, H, TOP]), ALU.mult).then_inc(s_pws, 1)
                elif r in R_DEC:
                    group = list(R_DEC).index(r)
                    h0, h1_ = R_DEC[r]
                    if group == 0:
                        dve.wait_ge(s_cst, CS * m + 8)
                        if young(1):
                            dve.wait_ge(s_ptp, n + 2)
                            dve.wait_ge(s_sm1, SM * n + 12)
                    for h in range(h0, h1_):
                        base = DEC * m + 3 * h + group
                        full = [128, TOP, NCAND]
                        if not (first(it) and h == 0):
                            dve.wait_ge(s_dst, base)
                        v.tensor_tensor(hot, fp[:, h, :].unsqueeze(2).to_broadcast(full), iota[:, :].unsqueeze(1).to_broadcast(full),
                                        ALU.is_equal).then_inc(s_dst, 1)
                        dve.wait_ge(s_dst, base + 1)
                        v.tensor_tensor(hot, hot, ci_[:, h, :].unsqueeze(1).to_broadcast(full), ALU.mult).then_inc(s_dst, 1)
                        dve.wait_ge(s_dst, base + 2)
                        v.tensor_reduce(fx[:, h, :], hot, AX.X, ALU.add).then_inc(s_dst, 1)
                    dve.wait_ge(s_dst, DEC * m + 3 * h1_ + group)
                    v.tensor_copy(ix[:, j % 2, h0:h1_, :], fx[:, h0:h1_, :]).then_inc(s_dst, 1)
                elif r in R_SUM:
                    for q in range(*R_SUM[r]):
                        h, half = divmod(q, 2)
                        if q == 0:
                            dve.wait_ge(s_pws, PW * m + 4)
                            if not is_cls:
                                dve.wait_ge(s_ktp, m)
                                dve.wait_ge(s_vf, m)
                        slot = q % GRING
                        dve.wait_ge(s_g[q], 16 * HALF * (m + 1))
                        rows8 = gg[:, slot, :, :]
                        v.tensor_tensor(rows8, rows8, pwt[:, j % 2, h, HALF * half:HALF * half + HALF].unsqueeze(2)
                                        .to_broadcast([128, HALF, 128]), ALU.mult).then_inc(s_mul, 1)
                        dve.wait_ge(s_mul, 2 * H * m + q + 1)
                        if half and not (first(it) and h == 0):
                            dve.wait_ge(s_kv, H * m + h)
                        v.tensor_reduce(kvh[:, :, :] if half else kv[:, :, h, :],
                                        rows8.rearrange("t k (w d) -> t w d k", w=2), AX.X, ALU.add)\
                            .then_inc(s_red, 1)
                        if half:
                            dve.wait_ge(s_red, 2 * H * m + q + 1)
                            v.tensor_tensor(kv[:, :, h, :], kv[:, :, h, :], kvh[:, :, :], ALU.add).then_inc(s_kv, 1)
                elif r == R_KT:
                    dve.wait_ge(s_kv, H * m + H)
                    if old(1):
                        dve.wait_ge(s_pv2, n)
                    v.tensor_copy((vc if is_cls else vf)[:, :, :], kv[:, 1, :, :]).then_inc(s_vf, 1)
                elif r == R_SC2 and not is_cls:
                    dve.wait_ge(s_sc2, n + 1)
                    dve.wait_ge(s_dst, DEC * m + DEC * (2 if young(1) else 1))
                    for e in range(2):
                        v.tensor_tensor(ee[:, :, 0:128].rearrange("t (c e) s -> t c e s", e=2)[:, :, e, :],
                                        wide[:, 512 * e:512 * e + 512].rearrange("t (c s) -> t c s", c=4),
                                        mask[:, :].unsqueeze(1).to_broadcast([128, 4, 128]), ALU.add)
                    v.tensor_copy(ee[:, :, 128], b5[:, 0:H]).then_inc(s_sm2, 1)
                    shift(it, 1, n, s_sm2)
                elif r == R_PT2 and not is_cls:
                    shares(1, n, s_ex2, s_sm2)
                elif r == R_PV2 and not is_cls:
                    dve.wait_ge(s_pv2, n + 1)
                    dve.wait_ge(s_sm2, SM * n + 6)
                    full = [128, H, D2]
                    if young(1):
                        dve.wait_ge(s_cst, CS * m + 2 * CS)
                    if young(2):
                        dve.wait_ge(s_ao, 3 * n + 9)
                    v.tensor_tensor(ftmp[:, :, :], vc[:, :, :], smx[:, 1, 3, :].unsqueeze(2).to_broadcast(full), ALU.mult)
                    if young(2):
                        dve.wait_ge(s_aop, m + 3)
                    v.tensor_tensor(fo[:, :, :], b5[:, :].rearrange("t (h d) -> t h d", h=H),
                                    smx[:, 1, 2, :].unsqueeze(2).to_broadcast(full), ALU.mult).then_inc(s_fo, 1)
                    dve.wait_ge(s_fo, 2 * n + 1)
                    v.tensor_tensor(fo[:, :, :], fo[:, :, :], ftmp[:, :, :], ALU.add).then_inc(s_fo, 1)
                elif r == R_WO2:
                    dve.wait_ge(s_wo2, m + 1)
                    if not is_cls:
                        e = j % 2
                        dve.wait_ge(s_out[e], 32 * (2 * (it - 1) + j // 2) + 16)
                    v.tensor_tensor(ob[:, j % 2, :], h1[:, j % PAIRS, :], b5[:, 0:SIDE], ALU.add).then_inc(s_ob, 1)

            def body(it, units, fno, tail):
                def middle(now):
                    for j, r, is_cls in tiles(it, now, tail):
                        tile_middle(it, j, r, is_cls)

                def late(now):
                    for bulk in (False, True):
                        for j, r, is_cls in tiles(it, now, tail):
                            if (r in R_DEC or r in R_SUM) == bulk:
                                tile(it, j, r, is_cls)

                for u in range(units):
                    now, later = steps(u, fno)
                    if fno:
                        unit(it, u, lambda: middle(now))
                    else:
                        middle(now)
                    late(now)
                    if fno:
                        unit_end(it, u)
                    middle(later)
                    late(later)

            iterations(dve, body)


def constants():
    f = np.float64
    ft = np.zeros((128, 32, 128), f)
    i1 = np.zeros((128, 32, 128), f)
    y8, x16 = np.divmod(np.arange(128), 16)
    a, b = np.divmod(np.arange(64), 8)
    for p in range(2):
        for q in range(2):
            for j in range(2):
                for px in range(2):
                    for py in range(2):
                        y, x = 2 * (8 * j + y8) + py, 2 * x16 + px
                        th = 2 * np.pi / SIDE * (np.outer(y, 2 * a + p) + np.outer(x, 2 * b + q))
                        ft[:, 8 * (2 * p + q) + 4 * j + 2 * px + py] = np.concatenate([np.cos(th), -np.sin(th)], 1)
    qi, rem = np.divmod(np.arange(128), 64)
    ai, bi = np.divmod(rem, 8)
    ky = 2 * bi + qi
    y4, rest = np.divmod(np.arange(128), 32)
    kyo, ro = np.divmod(rest, 2)
    same = ky[:, None] == kyo[None, :]
    for p in range(2):
        kx = 2 * ai + p
        for ri in range(2):
            for c in range(4):
                for py in range(2):
                    y = 2 * (4 * c + y4) + py
                    th = 2 * np.pi / SIDE * np.outer(kx, y)
                    if ri == 0:
                        w = np.where(ro[None, :] == 0, np.cos(th), np.sin(th))
                    else:
                        w = np.where(ro[None, :] == 0, -np.sin(th), np.cos(th))
                    i1[:, 8 * (2 * p + ri) + 2 * c + py] = w * same / SIDE
    i2 = np.zeros((128, 2, 128), f)
    yo, xo = np.divmod(np.arange(128), BLK)
    for px in range(2):
        th = 2 * np.pi / SIDE * np.outer(kyo, 2 * xo + px)
        w = np.where(ro[:, None] == 0, np.cos(th), -np.sin(th)) * np.where(kyo[:, None] == 0, 1, 2) / SIDE
        i2[:, px] = w * (y4[:, None] == yo[None, :])
    t = np.arange(128)
    seen = (t[:, None] // SIDE == t[None, :] // SIDE) & (t[None, :] <= t[:, None])
    rel = np.stack([np.where(seen, t[None, :] - t[:, None], NEG), np.where(seen, 0, NEG)])
    relcls = -(t[:, None] % SIDE + 1) * 0.5 ** (np.arange(H) + 1)[None, :]
    cst = {"ft_c": ft, "i1_c": i1, "i2_c": i2, "ident_c": np.eye(128), "rel_c": rel, "relcls_c": relcls,
           "iota_c": np.tile(np.arange(NCAND), (128, 1)), "head_c": np.tile(np.arange(H) * KEYS * KEYS, (128, 1))}
    return {k: np.ascontiguousarray(w.astype(np.float32)) for k, w in cst.items()}


def by_class(w):
    n = w.shape[0]
    w = w.reshape(n, CH, CH, 8, 2, 8, 2).transpose(0, 4, 1, 6, 3, 5, 2)
    return w.reshape(n, 2, CH, HM, CH)


def kernel(**inputs):
    import concourse.bacc as bacc
    from concourse.bass_utils import run_bass_kernel_spmd

    g = {k: np.asarray(w) for k, w in inputs.items()}
    x = g["x"].reshape(IMGS, BLK, 2, BLK, 2, 3).transpose(0, 4, 2, 5, 1, 3).reshape(IMGS, 12, BLK * BLK)
    grid = g["L0_tok_input_grid"].reshape(BLK, 2, BLK, 2, 2).transpose(3, 1, 4, 0, 2).reshape(8, BLK * BLK)
    wr_, wi_ = by_class(g["L0_tok_spec_wr"]), by_class(g["L0_tok_spec_wi"])
    wl = np.stack([np.stack([wr_, wi_], 4), np.stack([wi_, wr_], 4)], 2)
    wl = wl.reshape(LAYERS, 128, 4, 32, 2 * CH).transpose(0, 1, 3, 2, 4).reshape(LAYERS, 128, HM * 2 * CH)
    arrays = {
        "x12": x, "grid8": grid, "pw": g["L0_tok_P_w"], "pb": g["L0_tok_P_b"], "wl": wl,
        "cwt": g["L0_tok_conv_w"].transpose(3, 4, 2, 0, 1), "cb": g["L0_tok_conv_b"],
        "q1w": g["L0_tok_Q1_w"], "q1b": g["L0_tok_Q1_b"], "q2w": g["L0_tok_Q2_w"], "q2b": g["L0_tok_Q2_b"],
        "cls": g["cls_tok"], "wq": g["L0_attn_Wq"], "wk": g["L0_attn_Wk"], "wv": g["L0_attn_Wv"],
        "wo": g["L0_attn_Wo"], "bo": g["L0_attn_bo"], "wqpk": g["L0_ffn_Wq_pk"],
        "keyst": g["L0_ffn_pk_keys"].transpose(0, 2, 3, 1), "wq2": g["L0_ffn_Wq"],
        "table": np.concatenate([g["L0_ffn_keys_table"], g["L0_ffn_values_table"]], 1), "wo2": g["L0_ffn_Wo"],
    } | constants()

    nc = bacc.Bacc("TRN2", target_bir_lowering=False, num_devices=1)
    nc.disable_value_cache = True
    maps, args = {}, {}
    for name, a in arrays.items():
        a = np.ascontiguousarray(a)
        maps[f"in_{name}"] = a
        args[name] = nc.dram_tensor(f"in_{name}", a.shape, mybir.dt.from_np(a.dtype), kind="ExternalInput").ap()
    args["out"] = nc.dram_tensor("out_tokens", (IMGS, SIDE + 1, SIDE), F32, kind="ExternalOutput").ap()
    tower_kernel(nc, **args)
    r = run_bass_kernel_spmd(nc, [maps], core_ids=[0])
    return r.results[0]["out_tokens"]
```
